# Optimizing a Trainium2 kernel written in Bass

```python
import numpy as np
import jax
import jax.numpy as jnp

def _softmax(x, axis=-1):
    return jax.nn.softmax(x, axis=axis)

def _gelu(x):
    return jax.nn.gelu(x, approximate=True)

def _silu(x):
    return jax.nn.silu(x)

def _sigmoid(x):
    return jax.nn.sigmoid(x)

def _layernorm(x, axis=-1, eps=1e-05):
    m = jnp.mean(x, axis=axis, keepdims=True)
    v = jnp.var(x, axis=axis, keepdims=True)
    return (x - m) / jnp.sqrt(v + eps)

def _scatter_add(tgt, idx, src, axis=0):
    return tgt.at[idx].add(src)

def _segment_sum(src, seg, n):
    return jax.ops.segment_sum(src, seg, n)
kernel_name = 'mk_flamingo_gated_d1_seqx_r8_fd40aa'

def setup_inputs(seed: int=0):
    np.random.seed(seed)
    _w = jnp.asarray

    def _rec_inputs():
        import jax
        import jax.numpy as jnp
        _rk = jax.random.key(seed)
        x = -0.0002928 + 1 * jax.random.normal(jax.random.fold_in(_rk, 1), (32, 128, 128), jnp.float32)
        _lenS = 128 - jax.random.randint(jax.random.fold_in(_rk, 7), (32,), 0, max(1, 128 // 4) + 1, jnp.int32)
        _lenS2 = 128 - jax.random.randint(jax.random.fold_in(_rk, 8), (32,), 0, max(1, 128 // 4) + 1, jnp.int32)
        _ctx_1024P = jax.random.normal(jax.random.fold_in(_rk, 11), (32, 16, 128), jnp.float32)
        _ctx_1024c = jax.random.dirichlet(jax.random.fold_in(_rk, 511), 0.3 * jnp.ones((16,), jnp.float32), (32, 128))
        _ctx_1024t = jnp.einsum('bsk,bkd->bsd', _ctx_1024c, _ctx_1024P)
        _ctx_1024t = _ctx_1024t * jax.lax.rsqrt(jnp.mean(jnp.square(_ctx_1024t)) + 1e-12) * 0.953939
        ctx_1024 = -1.39393e-06 + 0.999914 * (_ctx_1024t + 0.3 * jax.random.normal(jax.random.fold_in(_rk, 611), (32, 128, 128), jnp.float32))
        _g = jax.random.normal(jax.random.fold_in(_rk, 9001), (2, 1), jnp.float32)
        _g = jnp.sign(_g) * jnp.maximum(jnp.abs(_g), 1.0) + (_g == 0) * 1.0
        g_xattn = _g[0]
        g_ffn = _g[1]
        return (x, ctx_1024, g_xattn, g_ffn)
    x, ctx_1024, g_xattn, g_ffn = _rec_inputs()

    def _L0_xattn_setup():
        import jax, jax.numpy as jnp
        import numpy as np
        D_MODEL = 64
        N_HEADS = 8
        D_KEYS = D_MODEL // N_HEADS
        DIN = D_MODEL * 2
        DPROJ = D_KEYS * N_HEADS * 2
        B, L = (2, 256)
        key = jax.random.key(seed)
        ks = jax.random.split(key, 11)
        s_in = 1.0 / np.sqrt(DIN)
        s_out = 1.0 / np.sqrt(DPROJ)
        return {'queries': jax.random.normal(ks[0], (B, L, DIN), jnp.float32), 'keys': jax.random.normal(ks[1], (B, L, DIN), jnp.float32), 'values': jax.random.normal(ks[2], (B, L, DIN), jnp.float32), 'Wq': jax.random.normal(ks[3], (DPROJ, DIN), jnp.float32) * s_in, 'bq': jax.random.normal(ks[4], (DPROJ,), jnp.float32) * s_in, 'Wk': jax.random.normal(ks[5], (DPROJ, DIN), jnp.float32) * s_in, 'bk': jax.random.normal(ks[6], (DPROJ,), jnp.float32) * s_in, 'Wv': jax.random.normal(ks[7], (DPROJ, DIN), jnp.float32) * s_in, 'bv': jax.random.normal(ks[8], (DPROJ,), jnp.float32) * s_in, 'Wo': jax.random.normal(ks[9], (DIN, DPROJ), jnp.float32) * s_out, 'bo': jax.random.normal(ks[10], (DIN,), jnp.float32) * s_out}
    _L0_xattn_all = _L0_xattn_setup()
    _L0_xattn_in = {k: v for k, v in _L0_xattn_all.items() if k in ('Wq', 'bq', 'Wk', 'bk', 'Wv', 'bv', 'Wo', 'bo')}
    del _L0_xattn_all

    def _L0_ffn_setup():
        import jax, jax.numpy as jnp
        import numpy as np
        LN_EPS = 1e-05

        def _swiglu(h, w_gate_up, w_down):
            gu = h @ w_gate_up.T
            gate, up = jnp.split(gu, 2, axis=-1)
            return jax.nn.silu(gate) * up @ w_down.T
        key = jax.random.key(seed)
        ks = jax.random.split(key, 6)
        d_model, d_ff, E = (128, 512, 8)
        shared_d_ff = d_ff // 4
        routed_d_ff = d_ff - shared_d_ff
        B, S = (4, 256)
        x = jax.random.normal(ks[0], (B, S, d_model), dtype=jnp.float32)
        ln_gamma = jnp.ones((d_model,), jnp.float32)
        ln_beta = jnp.zeros((d_model,), jnp.float32)
        router_w = jax.random.normal(ks[1], (E, d_model), jnp.float32) * 0.02
        gate_up_w = jax.random.normal(ks[2], (E, 2 * routed_d_ff, d_model), jnp.float32) * (1.0 / np.sqrt(d_model))
        down_w = jax.random.normal(ks[3], (E, d_model, routed_d_ff), jnp.float32) * (1.0 / np.sqrt(routed_d_ff))
        shared_gate_up_w = jax.random.normal(ks[4], (2 * shared_d_ff, d_model), jnp.float32) * (1.0 / np.sqrt(d_model))
        shared_down_w = jax.random.normal(ks[5], (d_model, shared_d_ff), jnp.float32) * (1.0 / np.sqrt(shared_d_ff))
        return dict(x=x, ln_gamma=ln_gamma, ln_beta=ln_beta, router_w=router_w, gate_up_w=gate_up_w, down_w=down_w, shared_gate_up_w=shared_gate_up_w, shared_down_w=shared_down_w)
    _L0_ffn_all = _L0_ffn_setup()
    _L0_ffn_in = {k: v for k, v in _L0_ffn_all.items() if k in ('ln_gamma', 'ln_beta', 'router_w', 'gate_up_w', 'down_w', 'shared_gate_up_w', 'shared_down_w')}
    del _L0_ffn_all
    return {'x': x, 'ctx_1024': ctx_1024, 'g_xattn': g_xattn, 'g_ffn': g_ffn, 'L0_xattn_Wq': _L0_xattn_in['Wq'], 'L0_xattn_bq': _L0_xattn_in['bq'], 'L0_xattn_Wk': _L0_xattn_in['Wk'], 'L0_xattn_bk': _L0_xattn_in['bk'], 'L0_xattn_Wv': _L0_xattn_in['Wv'], 'L0_xattn_bv': _L0_xattn_in['bv'], 'L0_xattn_Wo': _L0_xattn_in['Wo'], 'L0_xattn_bo': _L0_xattn_in['bo'], 'L0_ffn_ln_gamma': _L0_ffn_in['ln_gamma'], 'L0_ffn_ln_beta': _L0_ffn_in['ln_beta'], 'L0_ffn_router_w': _L0_ffn_in['router_w'], 'L0_ffn_gate_up_w': _L0_ffn_in['gate_up_w'], 'L0_ffn_down_w': _L0_ffn_in['down_w'], 'L0_ffn_shared_gate_up_w': _L0_ffn_in['shared_gate_up_w'], 'L0_ffn_shared_down_w': _L0_ffn_in['shared_down_w']}

def reference(x, ctx_1024, g_xattn, g_ffn, L0_xattn_Wq, L0_xattn_bq, L0_xattn_Wk, L0_xattn_bk, L0_xattn_Wv, L0_xattn_bv, L0_xattn_Wo, L0_xattn_bo, L0_ffn_ln_gamma, L0_ffn_ln_beta, L0_ffn_router_w, L0_ffn_gate_up_w, L0_ffn_down_w, L0_ffn_shared_gate_up_w, L0_ffn_shared_down_w):
    import jax
    import jax.numpy as jnp

    def _L0_xattn_ref(queries, keys, values, Wq, bq, Wk, bk, Wv, bv, Wo, bo):
        import jax, jax.numpy as jnp
        import numpy as np
        D_MODEL = 64
        N_HEADS = 8
        D_KEYS = D_MODEL // N_HEADS
        DIN = D_MODEL * 2
        DPROJ = D_KEYS * N_HEADS * 2
        B, L = (2, 256)
        b, l, _ = queries.shape
        H, E = (N_HEADS, 2)
        q = (queries @ Wq.T + bq).reshape(b, l, -1, H, E)
        k = (keys @ Wk.T + bk).reshape(b, l, -1, H, E)
        v = (values @ Wv.T + bv).reshape(b, l, -1, H, E)
        scale = 1.0 / np.sqrt(E)
        scores = jnp.einsum('bnlhe,bnshe->bnhls', q, k)
        A = jax.nn.softmax(scale * scores, axis=-1)
        out = jnp.einsum('bnhls,bnshd->bnlhd', A, v)
        out = out.reshape(b, l, -1)
        return out @ Wo.T + bo

    def _L0_ffn_ref(x, ln_gamma, ln_beta, router_w, gate_up_w, down_w, shared_gate_up_w, shared_down_w):
        import jax, jax.numpy as jnp
        import numpy as np
        LN_EPS = 1e-05

        def _swiglu(h, w_gate_up, w_down):
            gu = h @ w_gate_up.T
            gate, up = jnp.split(gu, 2, axis=-1)
            return jax.nn.silu(gate) * up @ w_down.T
        B, S, D = x.shape
        E = router_w.shape[0]
        top_k = 2
        xt = x.reshape(-1, D)
        mu = jnp.mean(xt, axis=-1, keepdims=True)
        var = jnp.mean(jnp.square(xt - mu), axis=-1, keepdims=True)
        normed = (xt - mu) * jax.lax.rsqrt(var + LN_EPS) * ln_gamma + ln_beta
        logits = normed.astype(jnp.float32) @ router_w.T
        probs = jax.nn.softmax(logits, axis=-1)
        top_v, top_i = jax.lax.top_k(probs, top_k)
        gates = jax.nn.softmax(top_v, axis=-1)
        comb = jnp.sum(jax.nn.one_hot(top_i, E, dtype=gates.dtype) * gates[..., None], axis=1)
        out = jnp.zeros_like(normed)
        for e in range(E):
            y = _swiglu(normed, gate_up_w[e], down_w[e])
            out = out + comb[:, e, None] * y
        out = out + _swiglu(normed, shared_gate_up_w, shared_down_w)
        return out.reshape(B, S, D)
    x = x + jnp.tanh(g_xattn[0]) * _L0_xattn_ref(_layernorm(x, axis=-1), ctx_1024, ctx_1024, L0_xattn_Wq, L0_xattn_bq, L0_xattn_Wk, L0_xattn_bk, L0_xattn_Wv, L0_xattn_bv, L0_xattn_Wo, L0_xattn_bo)
    x = x + jnp.tanh(g_ffn[0]) * _L0_ffn_ref(_layernorm(x, axis=-1), L0_ffn_ln_gamma, L0_ffn_ln_beta, L0_ffn_router_w, L0_ffn_gate_up_w, L0_ffn_down_w, L0_ffn_shared_gate_up_w, L0_ffn_shared_down_w)
    return x

_drawn_inputs = setup_inputs


def setup_inputs(seed=0):
    import zlib

    import numpy as np

    out = dict(_drawn_inputs(seed))
    spreads = {'L0_ffn_ln_gamma': (1.0, 0.2), 'L0_ffn_ln_beta': (0.0, 0.1)}
    factors = {}
    for name, (base, spread) in spreads.items():
        noise = np.random.default_rng([zlib.crc32(name.encode()), seed]).standard_normal(out[name].shape)
        drawn = base * np.exp(spread * noise) if base else spread * noise
        out[name] = jnp.asarray(drawn.astype(out[name].dtype))
    for name, factor in factors.items():
        out[name] = (out[name] * factor).astype(out[name].dtype)
    return out
```

```python
import numpy as np

import concourse.bass as bass
from concourse import mybir
from contextlib import ExitStack

FP32 = mybir.dt.float32
BF16 = mybir.dt.bfloat16
ALU = mybir.AluOpType
ACT = mybir.ActivationFunctionType
AX = mybir.AxisListType

B = 32
L = 128
D = 128
N, H, E2 = 8, 8, 2
NH = N * H
PAIRS = N * H * N
EPS = 1e-5
SM_SCALE = 1.0 / np.sqrt(E2)
EXPERTS = 8
F = 384
FS = 128
FC = F // 128
SLOTS = 4
FIRST, LAST = 3, 27


def attention_then_moe(nc, t):
    ctx = ExitStack()
    with ctx:
        def sb(name, shape, dt=FP32):
            return ctx.enter_context(nc.sbuf_tensor(name, shape, dt))

        def ps(name, shape, dt=FP32):
            return ctx.enter_context(nc.psum_tensor(name, shape, dt))

        def sem(name):
            return ctx.enter_context(nc.semaphore(name))

        def sems(name):
            return [sem(f"{name}{i}") for i in range(SLOTS)]

        x1_dram = nc.dram_tensor("x1_dram", [B, L, D], FP32).ap()
        nT_dram = nc.dram_tensor("nT_dram", [B, D, L], FP32).ap()
        lg_dram = nc.dram_tensor("lg_dram", [B, L, EXPERTS], FP32).ap()

        wq, wkv, wo = sb("wq_sb", [D, D]), sb("wkv_sb", [D, 2 * D]), sb("wo_sb", [D, D])
        bqkv_all = sb("bqkv_all", [L, 3 * D])
        bo_all = sb("bo_all", [L, D])
        gamma, beta = sb("gamma_sb", [D, 1]), sb("beta_sb", [D, 1])
        router = sb("router_sb", [D, EXPERTS])
        w_gu = sb("w_gu", [D, EXPERTS, 2 * F])
        w_dn = sb("w_dn", [128, EXPERTS * FC, D])
        ws_gu = sb("ws_gu", [D, 2 * FS])
        ws_dn = sb("ws_dn", [FS, D])
        gates_in = sb("gates_in", [L, 2])
        gates = sb("gates", [L, 2])
        ident = sb("ident", [128, 128])
        minus_half = sb("minus_half", [L, 1])

        def slots(name, shape):
            return [sb(f"{name}{i}", shape) for i in range(SLOTS)]

        xin, cin, xres = slots("xin", [L, D]), slots("cin", [L, D]), slots("xres", [L, D])
        stats, mv = slots("stats", [L, 6]), slots("mv", [L, 2])
        vareps, rstd, xn = slots("vareps", [L, 1]), slots("rstd", [L, 1]), slots("xn", [L, D])
        hcT = slots("hcT", [D, 2 * L])
        qkv = slots("qkv", [L, 3 * D])
        prod = slots("prod", [L, E2, PAIRS])
        smax = slots("smax", [L, NH])
        probs = slots("probs", [L, PAIRS])
        weighted = slots("weighted", [L, N, D])
        den, rden = slots("den", [L, NH]), slots("rden", [L, NH])
        attn, attnT = slots("attn", [L, D]), slots("attnT", [D, L])
        x1 = slots("x1_", [L, D])
        stats2, mv2 = slots("stats2_", [L, 6]), slots("mv2_", [L, 2])
        vareps2, rstd2, xhat = slots("vareps2_", [L, 1]), slots("rstd2_", [L, 1]), slots("xhat", [L, D])
        nT, lg = slots("nT", [D, L]), slots("lg", [L, EXPERTS])

        lg_all = sb("lg_all", [L, B, EXPERTS])
        comb = sb("comb", [L, B, EXPERTS])
        rt = [sb(f"rt{i}", [L, B, EXPERTS]) for i in range(4)]
        rs = [sb(f"rs{i}", [L, B]) for i in range(4)]
        iota_e = sb("iota_e", [L, EXPERTS])

        nTe = [sb(f"nTe{i}", [D, L]) for i in range(2)]
        x1e = [sb(f"x1e{i}", [L, D]) for i in range(2)]
        silu = [sb(f"silu{i}", [L, F]) for i in range(2)]
        hid = [sb(f"hid{i}", [L, F]) for i in range(2)]
        hidT = [sb(f"hidT{i}", [128, F]) for i in range(2)]
        out_sb = [sb(f"out_sb{i}", [L, D]) for i in range(2)]

        banks = [ps(f"bank{i}", [128, 512]) for i in range(4)]
        pairs = [ps(f"pair{i}", [128, 2, 512]) for i in range(2)]
        score_ps = banks[0:2]
        qkv_ps, xcT_ps = banks[2], banks[3]
        sum_ps, attnT_ps = pairs[0][:, 0, :], pairs[0][:, 1, :]
        oproj_ps, tail_ps = pairs[1][:, 0, :], pairs[1][:, 1, :]

        weights_in = sem("weights_in")
        bcast_in = sem("bcast_in")
        const_made = sem("const_made")
        ident_made = sem("ident_made")
        gates_done = sem("gates_done")
        bo_done = sem("bo_done")
        xc_in = sems("xc_in")
        xres_in = sems("xres_in")
        x1_out, nT_out, lg_out = sems("x1_out"), sems("nT_out"), sems("lg_out")
        stat_step = sem("stat_step")
        norm_step = sem("norm_step")
        xcT_ready = sem("xcT_ready")
        hcT_done = sem("hcT_done")
        qkv_ready = sem("qkv_ready")
        qkv_done = sem("qkv_done")
        prod0_done = sem("prod0_done")
        prod1_done = sem("prod1_done")
        scores_ready = sem("scores_ready")
        max_done = sem("max_done")
        shifted = sem("shifted")
        exp_done = sem("exp_done")
        den_done = sem("den_done")
        rden_done = sem("rden_done")
        weighted0_done = sem("weighted0_done")
        weighted1_done = sem("weighted1_done")
        sum_ready = sem("sum_ready")
        attn_done = sem("attn_done")
        attnT_ready = sem("attnT_ready")
        attnT_done = sem("attnT_done")
        oproj_ready = sem("oproj_ready")
        xres_done = sem("xres_done")
        x1_done = sem("x1_done")
        stat2_step = sem("stat2_step")
        norm2_step = sem("norm2_step")
        xhatT_ready = sem("xhatT_ready")
        nT_done = sem("nT_done")
        logits_ready = sem("logits_ready")
        lg_done = sem("lg_done")

        lg_in = sem("lg_in")
        route_step = sem("route_step")
        route_exp = sem("route_exp")
        comb_done = sem("comb_done")
        tile_in = [sem(f"tile_in{i}") for i in range(2)]
        gu_ready = sem("gu_ready")
        silu_done = sem("silu_done")
        hid_done = sem("hid_done")
        hidT_ready = sem("hidT_ready")
        hidT_done = sem("hidT_done")
        acc_ready = sem("acc_ready")
        out_done = sem("out_done")
        out_stored = [sem(f"out_stored{i}") for i in range(2)]

        block = ctx.enter_context(nc.Block())

        W_LOADS = 10

        class It:
            def __init__(self, i, r):
                self.i, self.r = i, r

            def of(self, off):
                return It(self.i, self.r + off)

            @property
            def slot(self):
                return self.r % SLOTS

            @property
            def b(self):
                return self.i * SLOTS + self.r

            def times(self, k, add=0):
                return self.i * (SLOTS * k) + (self.r * k + add)

            def round(self, k):
                return self.i * k + (self.r // SLOTS + 1) * k

            @property
            def inside(self):
                return not isinstance(self.i, int) or 0 <= self.b < B

        def scores_of(s, e):
            q = qkv[s][:, 0:D].rearrange("p (l h e) -> p l h e", l=N, h=H)[:, :, :, e]
            k = qkv[s][:, D:2 * D].rearrange("p (s h e) -> p h s e", s=N, h=H)[:, :, :, e]
            return (prod[s][:, e, :].rearrange("p (l h s) -> p l h s", l=N, h=H),
                    q.unsqueeze(3).broadcast_to([L, N, H, N]), k.unsqueeze(1).broadcast_to([L, N, H, N]))

        def weighted_of(s, e):
            p = probs[s][:, :].rearrange("p (l h s) -> p s l h", l=N, h=H)
            v = qkv[s][:, 2 * D:3 * D].rearrange("p (s h e) -> p s h e", s=N, h=H)[:, :, :, e]
            return (weighted[s][:, :, :].rearrange("p s (l h e) -> p s l h e", l=N, h=H)[:, :, :, :, e],
                    p, v.unsqueeze(2).broadcast_to([L, N, N, H]))

        spare = {}

        def own_wait(eng, semaphore, value):
            if not isinstance(value, int):
                if eng.engine not in spare:
                    spare[eng.engine] = eng.alloc_register(f"spare{len(spare)}")
                eng.reg_mov(spare[eng.engine], value)
                eng.wait_ge(ident_made, 1)
                value = spare[eng.engine]
            eng.wait_ge(semaphore, value)

        def every_iteration(eng, body):
            for b in range(-4, FIRST):
                body(It(0, b))
            with eng.Fori(0, (LAST - FIRST) // SLOTS) as i:
                for r in range(FIRST, FIRST + SLOTS):
                    body(It(i, r))
            for b in range(LAST, B + 2):
                body(It(0, b))

        @block.sync
        def _(sp):
            for dst, src in ((wq, t["wq"]), (wkv, t["wkv"]), (wo, t["wo"]),
                             (gamma, t["gamma"]), (beta, t["beta"]), (router, t["router"]),
                             (ws_gu, t["ws_gu"]), (ws_dn, t["ws_dn"])):
                sp.dma_start(dst[:, :], src).then_inc(weights_in, 16)
            sp.dma_start(w_gu[:, :, :], t["w_gu"]).then_inc(weights_in, 16)
            sp.dma_start(w_dn[:, :, :], t["w_dn"]).then_inc(weights_in, 16)

            def body(it):
                ld = it.of(4)
                if ld.inside:
                    if it.inside:
                        own_wait(sp, xcT_ready, it.times(1, 1))
                    sp.dma_start(xin[ld.slot][:, :], t["x"][ld.b]).then_inc(xc_in[ld.slot], 16)
                    sp.dma_start(cin[ld.slot][:, :], t["ctx"][ld.b]).then_inc(xc_in[ld.slot], 16)
                if it.inside:
                    sp.dma_start(xres[it.slot][:, :], t["x"][it.b]).then_inc(xres_in[it.slot], 16)
                ta = it.of(-1)
                if ta.inside:
                    sp.wait_ge(x1_done, ta.times(1, 1))
                    sp.dma_start(x1_dram[ta.b], x1[ta.slot][:, :]).then_inc(x1_out[ta.slot], 16)
                ta = it.of(-2)
                if ta.inside:
                    sp.wait_ge(nT_done, ta.times(1, 1))
                    sp.dma_start(nT_dram[ta.b], nT[ta.slot][:, :]).then_inc(nT_out[ta.slot], 16)
                    sp.wait_ge(lg_done, ta.times(1, 1))
                    sp.dma_start(lg_dram[ta.b], lg[ta.slot][:, :]).then_inc(lg_out[ta.slot], 16)

            every_iteration(sp, body)

            for s in range(SLOTS):
                for done in (x1_out, nT_out, lg_out):
                    sp.wait_ge(done[s], 16 * (B // SLOTS))
            sp.dma_start(lg_all[:, :, :], lg_dram.rearrange("b l e -> l b e")).then_inc(lg_in, 16)

            def load_tile(i, k, first):
                if not first:
                    sp.wait_ge(out_done, 2 * i + k - 1)
                sp.dma_start(nTe[k][:, :], nT_dram[2 * i + k]).then_inc(tile_in[k], 16)
                sp.dma_start(x1e[k][:, :], x1_dram[2 * i + k]).then_inc(tile_in[k], 16)

            def store_tile(i, k):
                sp.wait_ge(out_done, 2 * i + k + 1)
                sp.dma_start(t["out"][2 * i + k], out_sb[k][:, :]).then_inc(out_stored[k], 16)

            load_tile(0, 0, True)
            load_tile(0, 1, True)
            with sp.Fori(1, B // 2) as i:
                for k in range(2):
                    load_tile(i, k, False)
                    store_tile(i - 1, k)
            store_tile(B // 2 - 1, 0)
            store_tile(B // 2 - 1, 1)
            for k in range(2):
                sp.wait_ge(out_stored[k], 16 * (B // 2))

        @block.gpsimd
        def _(pool):
            pool.memset(ident[:, :], 0.0).then_inc(const_made, 1)
            pool.memset(minus_half[:, :], -0.5).then_inc(const_made, 1)
            pool.wait_ge(const_made, 2)
            pool.affine_select(out=ident[:, :], in_=ident[:, :], compare_op=ALU.not_equal, fill=1.0, base=0,
                               pattern=[[-1, 128]], channel_multiplier=1).then_inc(ident_made, 1)
            for dst, src in ((bqkv_all[:, :], t["bqkv"]), (bo_all[:, :], t["bo"])):
                pool.dma_start(dst, src.broadcast_to([L, src.shape[-1]])).then_inc(bcast_in, 16)
            for k in range(2):
                pool.dma_start(gates_in[:, k:k + 1], t["g"][:, k:k + 1].broadcast_to([L, 1])).then_inc(bcast_in, 16)
            pool.wait_ge(bcast_in, 64)
            pool.wait_ge(gates_done, 1)
            pool.tensor_scalar(bo_all[:, :], bo_all[:, :], gates[:, 0:1], None, ALU.mult).then_inc(bo_done, 1)
            pool.wait_ge(bo_done, 1)

            def body(it):
                if it.of(1).inside:
                    s, n = it.of(1).slot, it.of(1)
                    pool.wait_ge(qkv_done, n.times(1, 1))
                    pool.tensor_tensor(*scores_of(s, 1), ALU.mult).then_inc(prod1_done, 1)
                if it.of(3).inside:
                    s, n = it.of(3).slot, it.of(3)
                    own_wait(pool, stat_step, n.times(2, 2))
                    pool.tensor_scalar(vareps[s][:, :], mv[s][:, 1:2], EPS, None, ALU.add).then_inc(norm_step, 1)
                    pool.wait_ge(norm_step, n.times(3, 1))
                    pool.tensor_tensor(rstd[s][:, :], vareps[s][:, :], minus_half[:, :], ALU.pow).then_inc(norm_step, 1)
                    own_wait(pool, norm_step, n.times(3, 2))
                    pool.tensor_scalar(xn[s][:, :], xin[s][:, :], mv[s][:, 0:1], rstd[s][:, 0:1],
                                       ALU.subtract, ALU.mult).then_inc(norm_step, 1)
                if it.inside:
                    s = it.slot
                    pool.wait_ge(exp_done, it.times(1, 1))
                    pool.tensor_tensor(*weighted_of(s, 1), ALU.mult).then_inc(weighted1_done, 1)
                    pool.wait_ge(xres_in[s], it.round(16))
                    pool.tensor_tensor(xres[s][:, :], xres[s][:, :], bo_all[:, :], ALU.add).then_inc(xres_done, 1)
                if it.of(-1).inside:
                    s, n = it.of(-1).slot, it.of(-1)
                    own_wait(pool, stat2_step, n.times(2, 2))
                    pool.tensor_scalar(vareps2[s][:, :], mv2[s][:, 1:2], 1.0 + EPS, EPS * EPS, ALU.mult, ALU.add)\
                        .then_inc(norm2_step, 1)
                    pool.wait_ge(norm2_step, n.times(3, 1))
                    pool.tensor_tensor(rstd2[s][:, :], vareps2[s][:, :], minus_half[:, :], ALU.pow).then_inc(norm2_step, 1)
                    own_wait(pool, norm2_step, n.times(3, 2))
                    pool.tensor_scalar(xhat[s][:, :], x1[s][:, :], mv2[s][:, 0:1], rstd2[s][:, 0:1],
                                       ALU.subtract, ALU.mult).then_inc(norm2_step, 1)

            every_iteration(pool, body)

        @block.tensor
        def _(pe):
            pe.wait_ge(weights_in, W_LOADS * 16)
            pe.wait_ge(ident_made, 1)

            def body(it):
                if it.of(-1).inside:
                    n = it.of(-1)
                    pe.wait_ge(attn_done, n.times(1, 1))
                    if n.of(-1).inside:
                        pe.wait_ge(attnT_done, n.times(1))
                    pe.transpose(attnT_ps[:, 0:128], attn[n.slot][:, :], ident[:, :]).then_inc(attnT_ready, 1)
                if it.of(-2).inside:
                    n = it.of(-2)
                    pe.wait_ge(norm2_step, n.times(3, 3))
                    if n.of(-1).inside:
                        pe.wait_ge(lg_done, n.times(1))
                    pe.transpose(tail_ps[:, 0:128], xhat[n.slot][:, :], ident[:, :]).then_inc(xhatT_ready, 1)
                if it.of(2).inside:
                    n = it.of(2)
                    pe.wait_ge(xc_in[n.slot], n.round(32))
                    pe.wait_ge(norm_step, n.times(3, 3))
                    if n.of(-1).inside:
                        pe.wait_ge(hcT_done, n.times(1))
                    pe.transpose(xcT_ps[:, 0:128], xn[n.slot][:, :], ident[:, :])
                    pe.transpose(xcT_ps[:, 128:256], cin[n.slot][:, :], ident[:, :]).then_inc(xcT_ready, 1)
                if it.of(1).inside:
                    n = it.of(1)
                    pe.wait_ge(prod0_done, n.times(1, 1))
                    pe.wait_ge(prod1_done, n.times(1, 1))
                    if n.of(-2).inside:
                        pe.wait_ge(shifted, n.times(1, -1))
                    pe.matmul(score_ps[n.r % 2][:, :], ident[:, :], prod[n.slot][:, 0, :], start=True, stop=False)
                    pe.matmul(score_ps[n.r % 2][:, :], ident[:, :], prod[n.slot][:, 1, :], start=False, stop=True)\
                        .then_inc(scores_ready, 1)
                if it.of(-1).inside:
                    n = it.of(-1)
                    pe.wait_ge(attnT_done, n.times(1, 1))
                    if n.of(-1).inside:
                        pe.wait_ge(x1_done, n.times(1))
                    pe.matmul(oproj_ps[:, 0:D], attnT[n.slot][:, :], wo[:, :], start=True, stop=True).then_inc(oproj_ready, 1)
                if it.of(-2).inside:
                    n = it.of(-2)
                    pe.wait_ge(nT_done, n.times(1, 1))
                    pe.matmul(tail_ps[:, 0:EXPERTS], nT[n.slot][:, :], router[:, :], start=True, stop=True)\
                        .then_inc(logits_ready, 1)
                if it.of(2).inside:
                    n = it.of(2)
                    pe.wait_ge(hcT_done, n.times(1, 1))
                    if n.of(-1).inside:
                        pe.wait_ge(qkv_done, n.times(1))
                    pe.matmul(qkv_ps[:, 0:D], hcT[n.slot][:, 0:L], wq[:, :], start=True, stop=True)
                    pe.matmul(qkv_ps[:, D:3 * D], hcT[n.slot][:, L:2 * L], wkv[:, :], start=True, stop=True).then_inc(qkv_ready, 1)
                if it.inside:
                    pe.wait_ge(weighted0_done, it.times(1, 1))
                    pe.wait_ge(weighted1_done, it.times(1, 1))
                    if it.of(-1).inside:
                        pe.wait_ge(attn_done, it.times(1))
                    for k in range(N):
                        last = pe.matmul(sum_ps[:, 0:D], ident[:, :], weighted[it.slot][:, k, :], start=(k == 0), stop=(k == N - 1))
                    last.then_inc(sum_ready, 1)

            every_iteration(pe, body)

            expert_list = [(w_gu[:, e, 0:F], w_gu[:, e, F:2 * F], [w_dn[:, e * FC + c, :] for c in range(FC)]) for e in range(EXPERTS)]
            expert_list.append((ws_gu[:, 0:FS], ws_gu[:, FS:2 * FS], [ws_dn[:, :]]))
            NE = len(expert_list)

            def gate_up(i, k, e, first):
                n = NE * k + e
                if e == 0:
                    pe.wait_ge(tile_in[k], 32 * (i + 1))
                if not (first and n < 2):
                    pe.wait_ge(hid_done, 2 * NE * i + n - 1)
                wg, wu, _ = expert_list[e]
                f = wg.shape[-1]
                pe.matmul(pairs[n % 2][:, 0, 0:f], nTe[k][:, :], wg, start=True, stop=True)
                pe.matmul(pairs[n % 2][:, 1, 0:f], nTe[k][:, :], wu, start=True, stop=True).then_inc(gu_ready, 1)

            def down(i, k, e, first):
                n = NE * k + e
                _, _, wd = expert_list[e]
                pe.wait_ge(hid_done, 2 * NE * i + n + 1)
                if not (first and n < 2):
                    pe.wait_ge(hidT_done, 2 * NE * i + n - 1)
                for c in range(len(wd)):
                    last = pe.transpose(banks[n % 2][:, c * 128:(c + 1) * 128], hid[n % 2][:, c * 128:(c + 1) * 128], ident[:, :])
                last.then_inc(hidT_ready, 1)

            def accumulate(i, k, e, first):
                n = NE * k + e
                _, _, wd = expert_list[e]
                acc = banks[2 + k][:, 0:D]
                pe.wait_ge(hidT_done, 2 * NE * i + n + 1)
                if e == 0 and not first:
                    pe.wait_ge(out_done, 2 * i + k - 1)
                for c in range(len(wd)):
                    last = pe.matmul(acc, hidT[n % 2][:, c * 128:(c + 1) * 128], wd[c],
                                     start=(e == 0 and c == 0), stop=(e == NE - 1 and c == len(wd) - 1))
                last.then_inc(acc_ready, 1)

            def tiles(i, first):
                for n in range(2 * NE):
                    gate_up(i, n // NE, n % NE, first)
                    if n >= 1:
                        down(i, (n - 1) // NE, (n - 1) % NE, first)
                    if n >= 2:
                        accumulate(i, (n - 2) // NE, (n - 2) % NE, first)
                down(i, 1, NE - 1, False)
                accumulate(i, 1, NE - 2, False)
                accumulate(i, 1, NE - 1, False)

            tiles(0, True)
            with pe.Fori(1, B // 2) as i:
                tiles(i, False)

        NE = EXPERTS + 1

        @block.scalar
        def _(act):
            act.wait_ge(bcast_in, 64)
            act.activation(gates[:, :], gates_in[:, :], ACT.Tanh).then_inc(gates_done, 1)
            act.wait_ge(weights_in, W_LOADS * 16)

            def body(it):
                if it.of(-1).inside:
                    n = it.of(-1)
                    act.wait_ge(attnT_ready, n.times(1, 1))
                    act.activation(attnT[n.slot][:, :], attnT_ps[:, 0:128], ACT.Copy).then_inc(attnT_done, 1)
                if it.of(-2).inside:
                    n = it.of(-2)
                    act.wait_ge(xhatT_ready, n.times(1, 1))
                    if n.of(-1).inside:
                        act.wait_ge(nT_out[n.of(-1).slot], n.of(-1).round(16))
                    act.activation(nT[n.slot][:, :], tail_ps[:, 0:128], ACT.Identity, bias=beta[:, 0:1], scale=gamma[:, 0:1])\
                        .then_inc(nT_done, 1)
                if it.of(2).inside:
                    n = it.of(2)
                    act.wait_ge(xcT_ready, n.times(1, 1))
                    act.activation(hcT[n.slot][:, :], xcT_ps[:, 0:256], ACT.Copy).then_inc(hcT_done, 1)
                if it.of(1).inside:
                    n = it.of(1)
                    act.wait_ge(shifted, n.times(1, 1))
                    act.activation(probs[n.slot][:, :], probs[n.slot][:, :], ACT.Exp, scale=SM_SCALE).then_inc(exp_done, 1)

            every_iteration(act, body)

            act.wait_ge(route_step, 2)
            act.activation(rt[1][:, :, :], rt[0][:, :, :], ACT.Exp).then_inc(route_exp, 1)
            act.wait_ge(route_step, ROUTE_GATE)
            act.activation(rs[3][:, :], rs[2][:, :], ACT.Exp).then_inc(route_exp, 1)

            def tiles(i, first):
                for n in range(2 * NE + 1):
                    if n < 2 * NE:
                        f = F if n % NE < EXPERTS else FS
                        act.wait_ge(gu_ready, 2 * NE * i + n + 1)
                        if not (first and n < 2):
                            act.wait_ge(hid_done, 2 * NE * i + n - 1)
                        act.activation(silu[n % 2][:, 0:f], pairs[n % 2][:, 0, 0:f], ACT.Silu).then_inc(silu_done, 1)
                    if n >= 1:
                        m = n - 1
                        f = F if m % NE < EXPERTS else FS
                        act.wait_ge(hidT_ready, 2 * NE * i + m + 1)
                        if not (first and m < 2):
                            act.wait_ge(acc_ready, 2 * NE * i + m - 1)
                        act.activation(hidT[m % 2][:, 0:f], banks[m % 2][:, 0:f], ACT.Copy).then_inc(hidT_done, 1)

            tiles(0, True)
            with act.Fori(1, B // 2) as i:
                tiles(i, False)

        @block.vector
        def _(dve):
            def body(it):
                def heads(ap):
                    return ap.rearrange("p (n e) -> p n e", e=E2)

                if it.of(-1).inside:
                    s, n = it.of(-1).slot, it.of(-1)
                    dve.wait_ge(sum_ready, n.times(1, 1))
                    dve.wait_ge(rden_done, n.times(1, 1))
                    dve.tensor_tensor(heads(attn[s][:, :]), heads(sum_ps[:, 0:D]), rden[s][:, :].unsqueeze(2).broadcast_to([L, NH, E2]),
                                      ALU.mult).then_inc(attn_done, 1)
                if it.of(1).inside:
                    s, n = it.of(1).slot, it.of(1)
                    dve.wait_ge(qkv_done, n.times(1, 1))
                    dve.tensor_tensor(*scores_of(s, 0), ALU.mult).then_inc(prod0_done, 1)
                if it.inside:
                    s = it.slot
                    dve.wait_ge(exp_done, it.times(1, 1))
                    dve.tensor_tensor(*weighted_of(s, 0), ALU.mult).then_inc(weighted0_done, 1)
                    dve.tensor_reduce(den[s][:, :], probs[s][:, :].rearrange("p (n s) -> p n s", s=N), AX.X, ALU.add).then_inc(den_done, 1)
                    dve.wait_ge(den_done, it.times(1, 1))
                    dve.reciprocal(rden[s][:, :], den[s][:, :]).then_inc(rden_done, 1)
                if it.of(1).inside:
                    s, n = it.of(1).slot, it.of(1)
                    by_s = score_ps[n.r % 2][:, :].rearrange("p (n s) -> p n s", s=N)
                    dve.wait_ge(scores_ready, n.times(1, 1))
                    dve.tensor_reduce(smax[s][:, :], by_s, AX.X, ALU.max).then_inc(max_done, 1)
                    dve.wait_ge(max_done, n.times(1, 1))
                    dve.tensor_tensor(probs[s][:, :].rearrange("p (n s) -> p n s", s=N), by_s,
                                      smax[s][:, :].unsqueeze(2).broadcast_to([L, NH, N]), ALU.subtract).then_inc(shifted, 1)
                if it.of(-1).inside:
                    s, n = it.of(-1).slot, it.of(-1)
                    dve.wait_ge(oproj_ready, n.times(1, 1))
                    dve.wait_ge(xres_done, n.times(1, 1))
                    if n.of(-1).inside:
                        dve.wait_ge(x1_out[n.of(-1).slot], n.of(-1).round(16))
                    dve.scalar_tensor_tensor(x1[s][:, :], oproj_ps[:, 0:D], gates[:, 0:1], xres[s][:, :], ALU.mult, ALU.add)\
                        .then_inc(x1_done, 1)
                    dve.wait_ge(x1_done, n.times(1, 1))
                    dve.bn_stats(stats2[s][:, :], x1[s][:, :]).then_inc(stat2_step, 1)
                    own_wait(dve, stat2_step, n.times(2, 1))
                    dve.bn_aggr(mv2[s][:, :], stats2[s][:, :]).then_inc(stat2_step, 1)
                if it.of(2).inside:
                    s, n = it.of(2).slot, it.of(2)
                    dve.wait_ge(qkv_ready, n.times(1, 1))
                    dve.tensor_tensor(qkv[s][:, :], qkv_ps[:, 0:3 * D], bqkv_all[:, :], ALU.add).then_inc(qkv_done, 1)
                if it.of(3).inside:
                    s, n = it.of(3).slot, it.of(3)
                    dve.wait_ge(xc_in[s], n.round(32))
                    dve.bn_stats(stats[s][:, :], xin[s][:, :]).then_inc(stat_step, 1)
                    own_wait(dve, stat_step, n.times(2, 1))
                    dve.bn_aggr(mv[s][:, :], stats[s][:, :]).then_inc(stat_step, 1)
                if it.of(-2).inside:
                    s, n = it.of(-2).slot, it.of(-2)
                    dve.wait_ge(logits_ready, n.times(1, 1))
                    if n.of(-1).inside:
                        dve.wait_ge(lg_out[n.of(-1).slot], n.of(-1).round(16))
                    dve.tensor_copy(lg[s][:, :], tail_ps[:, 0:EXPERTS]).then_inc(lg_done, 1)

            dve.wait_ge(gates_done, 1)
            dve.wait_ge(bcast_in, 64)
            every_iteration(dve, body)

            steps = [0]

            def step(ins):
                steps[0] += 1
                ins.then_inc(route_step, 1)
                dve.wait_ge(route_step, steps[0])

            def over_e(a):
                return a.unsqueeze(2).broadcast_to([L, B, EXPERTS])

            for e in range(EXPERTS):
                last = dve.memset(iota_e[:, e:e + 1], float(e - EXPERTS))
            iota = iota_e[:, :].unsqueeze(1).broadcast_to([L, B, EXPERTS])
            dve.wait_ge(lg_in, 16)
            step(dve.tensor_reduce(rs[0][:, :], lg_all[:, :, :], AX.X, ALU.max))
            step(dve.tensor_tensor(rt[0][:, :, :], lg_all[:, :, :], over_e(rs[0][:, :]), ALU.subtract))
            dve.wait_ge(route_exp, 1)
            step(dve.tensor_reduce(rs[0][:, :], rt[1][:, :, :], AX.X, ALU.add))
            step(dve.reciprocal(rs[1][:, :], rs[0][:, :]))
            step(dve.tensor_tensor(rt[0][:, :, :], rt[1][:, :, :], over_e(rs[1][:, :]), ALU.mult))

            def top(p, onehot, value, scratch, index):
                step(dve.tensor_reduce(value, p, AX.X, ALU.max))
                step(dve.tensor_tensor(scratch, p, over_e(value), ALU.is_equal))
                step(dve.tensor_tensor(scratch, scratch, iota, ALU.mult))
                step(dve.tensor_reduce(index, scratch, AX.X, ALU.min))
                step(dve.tensor_tensor(onehot, iota, over_e(index), ALU.is_equal))

            top(rt[0][:, :, :], rt[2][:, :, :], rs[0][:, :], rt[1][:, :, :], rs[2][:, :])
            step(dve.scalar_tensor_tensor(rt[3][:, :, :], rt[2][:, :, :], -2.0, rt[0][:, :, :], ALU.mult, ALU.add))
            top(rt[3][:, :, :], rt[0][:, :, :], rs[1][:, :], rt[1][:, :, :], rs[2][:, :])
            step(dve.tensor_tensor(rs[2][:, :], rs[1][:, :], rs[0][:, :], ALU.subtract))
            assert steps[0] == ROUTE_GATE
            dve.wait_ge(route_exp, 2)
            step(dve.tensor_scalar(rs[0][:, :], rs[3][:, :], 1.0, None, ALU.add))
            step(dve.reciprocal(rs[1][:, :], rs[0][:, :]))
            step(dve.tensor_tensor(rs[2][:, :], rs[1][:, :], rs[3][:, :], ALU.mult))
            step(dve.tensor_tensor(rt[1][:, :, :], rt[2][:, :, :], over_e(rs[1][:, :]), ALU.mult))
            step(dve.tensor_tensor(rt[3][:, :, :], rt[0][:, :, :], over_e(rs[2][:, :]), ALU.mult))
            dve.tensor_tensor(comb[:, :, :], rt[1][:, :, :], rt[3][:, :, :], ALU.add).then_inc(comb_done, 1)
            dve.wait_ge(comb_done, 1)

            def tiles(i, first):
                for n in range(2 * NE):
                    k, e = n // NE, n % NE
                    f = F if e < EXPERTS else FS
                    dve.wait_ge(silu_done, 2 * NE * i + n + 1)
                    if not (first and n < 2):
                        dve.wait_ge(hidT_ready, 2 * NE * i + n - 1)
                    if e < EXPERTS:
                        scale = comb[:, 2 * i + k, e:e + 1] if first else comb[:, :, :].rearrange("l b e -> l (b e)")[:, bass.ds((2 * i + k) * EXPERTS + e, 1)]
                        dve.scalar_tensor_tensor(hid[n % 2][:, 0:f], pairs[n % 2][:, 1, 0:f], scale, silu[n % 2][:, 0:f],
                                                 ALU.mult, ALU.mult).then_inc(hid_done, 1)
                    else:
                        dve.tensor_tensor(hid[n % 2][:, 0:f], pairs[n % 2][:, 1, 0:f], silu[n % 2][:, 0:f], ALU.mult).then_inc(hid_done, 1)
                    if n == NE + 2:
                        finish(i, 0, first)
                finish(i, 1, first)

            def finish(i, k, first):
                dve.wait_ge(acc_ready, 2 * NE * i + NE * (k + 1))
                if not first:
                    dve.wait_ge(out_stored[k], 16 * i)
                dve.scalar_tensor_tensor(out_sb[k][:, :], banks[2 + k][:, 0:D], gates[:, 1:2], x1e[k][:, :],
                                         ALU.mult, ALU.add).then_inc(out_done, 1)

            tiles(0, True)
            with dve.Fori(1, B // 2) as i:
                tiles(i, False)


ROUTE_GATE = 17


def kernel(**inputs):
    import concourse.bacc as bacc
    from concourse.bass_utils import run_bass_kernel_spmd

    a = {k: np.asarray(v) for k, v in inputs.items()}
    gu = a["L0_ffn_gate_up_w"]
    arrays = {
        "x": a["x"], "ctx": a["ctx_1024"],
        "g": np.concatenate([a["g_xattn"], a["g_ffn"]]).reshape(1, 2),
        "wq": a["L0_xattn_Wq"].T, "wkv": np.concatenate([a["L0_xattn_Wk"], a["L0_xattn_Wv"]]).T,
        "bqkv": np.concatenate([a["L0_xattn_bq"], a["L0_xattn_bk"], a["L0_xattn_bv"]]).reshape(1, 3 * D),
        "wo": a["L0_xattn_Wo"].T, "bo": a["L0_xattn_bo"].reshape(1, D),
        "gamma": a["L0_ffn_ln_gamma"].reshape(D, 1), "beta": a["L0_ffn_ln_beta"].reshape(D, 1),
        "router": a["L0_ffn_router_w"].T,
        "w_gu": gu.transpose(2, 0, 1),
        "w_dn": a["L0_ffn_down_w"].transpose(0, 2, 1).reshape(EXPERTS, FC, 128, D).transpose(2, 0, 1, 3).reshape(128, EXPERTS * FC, D),
        "ws_gu": a["L0_ffn_shared_gate_up_w"].T, "ws_dn": a["L0_ffn_shared_down_w"].T,
    }
    nc = bacc.Bacc("TRN2", target_bir_lowering=False, num_devices=1)
    fed, t = {}, {}
    for name, v in arrays.items():
        v = np.ascontiguousarray(v)
        fed[f"in_{name}"] = v
        t[name] = nc.dram_tensor(f"in_{name}", v.shape, mybir.dt.from_np(v.dtype), kind="ExternalInput").ap()
    t["out"] = nc.dram_tensor("out", [B, L, D], FP32, kind="ExternalOutput").ap()
    attention_then_moe(nc, t)
    r = run_bass_kernel_spmd(nc, [fed], core_ids=[0])
    return r.results[0]["out"]
```

```python
import numpy as np

import concourse.bass as bass
from concourse import mybir
from concourse.bass import IndirectOffsetOnAxis
from contextlib import ExitStack

FP32 = mybir.dt.float32
INT32 = mybir.dt.int32
ALU = mybir.AluOpType
ACT = mybir.ActivationFunctionType
AX = mybir.AxisListType

B = 32
L = 128
D = 128
N, H, E2 = 8, 8, 2
NH = N * H
PAIRS = N * H * N
EPS = 1e-5
SM_SCALE = 1.0 / np.sqrt(E2)
EXPERTS = 8
F = 384
FS = 128
FC = F // 128
TOKENS = B * L
TOP_K = 2
PAIRED = TOP_K * TOKENS
TILES = PAIRED // 128 + EXPERTS - 1
Y_ROWS = PAIRED + TILES * 128
SLOTS = 4
ROUND_UP = 1.5 * 2.0 ** 23


def attention_then_moe(nc, t):
    ctx = ExitStack()
    with ctx:
        def sb(name, shape, dt=FP32):
            return ctx.enter_context(nc.sbuf_tensor(name, shape, dt))

        def ps(name, shape, dt=FP32):
            return ctx.enter_context(nc.psum_tensor(name, shape, dt))

        def sem(name):
            return ctx.enter_context(nc.semaphore(name))

        def sems(name):
            return [sem(f"{name}{i}") for i in range(SLOTS)]

        x1_dram = nc.dram_tensor("x1_dram", [B, L, D], FP32).ap()
        xhat_dram = nc.dram_tensor("xhat_dram", [TOKENS, D], FP32).ap()
        y_dram = nc.dram_tensor("y_dram", [Y_ROWS, D], FP32).ap()
        nT_dram = nc.dram_tensor("nT_dram", [B, D, L], FP32).ap()
        lg_dram = nc.dram_tensor("lg_dram", [B, L, EXPERTS], FP32).ap()

        wq, wkv, wo = sb("wq_sb", [D, D]), sb("wkv_sb", [D, 2 * D]), sb("wo_sb", [D, D])
        bqkv_all = sb("bqkv_all", [L, 3 * D])
        bo = sb("bo_sb", [1, D])
        ones = sb("ones", [1, L])
        gamma, beta = sb("gamma_sb", [D, 1]), sb("beta_sb", [D, 1])
        router = sb("router_sb", [D, EXPERTS])
        w_gu = sb("w_gu", [D, EXPERTS, 2 * F])
        w_dn = sb("w_dn", [128, EXPERTS * FC, D])
        ws_gu = sb("ws_gu", [D, 2 * FS])
        ws_dn = sb("ws_dn", [FS, D])
        gates_in = sb("gates_in", [L, 2])
        gates = sb("gates", [L, 2])
        ident = sb("ident", [128, 128])
        minus_half = sb("minus_half", [L, 1])

        def slots(name, shape):
            return [sb(f"{name}{i}", shape) for i in range(SLOTS)]

        xin, cin, xres = slots("xin", [L, D]), slots("cin", [L, D]), slots("xres", [L, D])
        stats, mv = slots("stats", [L, 6]), slots("mv", [L, 2])
        vareps, rstd, xn = slots("vareps", [L, 1]), slots("rstd", [L, 1]), slots("xn", [L, D])
        hcT = slots("hcT", [D, 2 * L])
        qkv = slots("qkv", [L, 3 * D])
        prod = slots("prod", [L, E2, PAIRS])
        smax = slots("smax", [L, NH])
        probs = slots("probs", [L, PAIRS])
        weighted = slots("weighted", [L, N, D])
        den, rden = slots("den", [L, NH]), slots("rden", [L, NH])
        attn, attnT = slots("attn", [L, D]), slots("attnT", [D, L])
        x1 = slots("x1_", [L, D])
        stats2, mv2 = slots("stats2_", [L, 6]), slots("mv2_", [L, 2])
        vareps2, rstd2, xhat = slots("vareps2_", [L, 1]), slots("rstd2_", [L, 1]), slots("xhat", [L, D])
        nT, lg = slots("nT", [D, L]), slots("lg", [L, EXPERTS])

        lg_all = sb("lg_all", [L, B, EXPERTS])
        pair_gate = sb("pair_gate", [L, TOP_K * B])
        iota = sb("iota", [L, 128])
        before = sb("before", [128, 128])
        all_ones = sb("all_ones", [128, 128])
        pair_id = sb("pair_id", [L, TOP_K * B])
        pad_id = sb("pad_id", [L, TILES])
        PAD, PAD_E = B // 2, EXPERTS // 2
        count = [sb(f"count{i}", [L, PAD + B, EXPERTS]) for i in range(2)]
        tiles_of = [sb(f"tiles_of{i}", [L, PAD_E + EXPERTS]) for i in range(2)]
        count_over = sb("count_over", [L, EXPERTS, B])
        count_tiles = sb("count_tiles", [L, EXPERTS])
        first_row = sb("first_row", [L, EXPERTS])
        row = sb("row", [L, TOP_K, B])
        row_tile, row_in_tile = sb("row_tile", [L, TOP_K * B]), sb("row_in_tile", [L, TOP_K * B])
        zeros = sb("zeros", [128, TILES])
        onehot_in = [sb(f"onehot_in{i}", [128, 128]) for i in range(SLOTS)]
        onehot_tile = [sb(f"onehot_tile{i}", [128, TILES]) for i in range(SLOTS)]
        behind = sb("behind", [1, TILES, EXPERTS])
        tile_expert_f, tile_expert = sb("tile_expert_f", [1, TILES]), sb("tile_expert", [1, TILES], INT32)
        held = [sb(f"held{i}", [128, TILES]) for i in range(5)]
        from_row, to_row = sb("from_row", [128, TILES], INT32), sb("to_row", [128, TILES], INT32)
        rt = [sb(f"rt{i}", [L, B, EXPERTS]) for i in range(4)]
        rs = [sb(f"rs{i}", [L, B]) for i in range(4)]
        iota_e = sb("iota_e", [L, EXPERTS])

        from_now = [sb(f"from_now{i}", [128, 1], INT32) for i in range(SLOTS)]
        to_now = [sb(f"to_now{i}", [128, 1], INT32) for i in range(SLOTS)]
        xg = [sb(f"xg{i}", [128, D]) for i in range(SLOTS)]
        y = [sb(f"y{i}", [128, D]) for i in range(SLOTS)]
        nTe = [sb(f"nTe{i}", [D, L]) for i in range(2)]
        silu = [sb(f"silu{i}", [L, F]) for i in range(2)]
        hid = [sb(f"hid{i}", [L, F]) for i in range(2)]
        hidT = [sb(f"hidT{i}", [128, F]) for i in range(2)]
        nTf = [sb(f"nTf{i}", [D, L]) for i in range(SLOTS)]
        x1f = [sb(f"x1f{i}", [L, D]) for i in range(SLOTS)]
        yf = [[sb(f"yf{i}_{k}", [L, D]) for k in range(TOP_K)] for i in range(SLOTS)]
        out_sb = [sb(f"out_sb{i}", [L, D]) for i in range(SLOTS)]

        banks = [ps(f"bank{i}", [128, 512]) for i in range(4)]
        pairs = [ps(f"pair{i}", [128, 2, 512]) for i in range(2)]
        score_ps = banks[0:2]
        qkv_ps, xcT_ps = banks[2], banks[3]
        sum_ps, attnT_ps = pairs[0][:, 0, :], pairs[0][:, 1, :]
        oproj_ps, tail_ps = pairs[1][:, 0, :], pairs[1][:, 1, :]
        count_ps, held_ps = banks[2], banks[3]
        hidT_ps = banks[0:2]
        xgT_ps, down_ps = banks[2], banks[3]

        weights_in = sem("weights_in")
        bcast_in = sem("bcast_in")
        const_made = sem("const_made")
        ident_made = sem("ident_made")
        gates_done = sem("gates_done")
        xc_in = sems("xc_in")
        xres_in = sems("xres_in")
        xhat_out = sems("xhat_out")
        x1_out, nT_out, lg_out = sems("x1_out"), sems("nT_out"), sems("lg_out")
        stat_step = sem("stat_step")
        norm_step = sem("norm_step")
        xn_done = sem("xn_done")
        xcT_ready = sem("xcT_ready")
        hcT_done = sem("hcT_done")
        qkv_ready = sem("qkv_ready")
        qkv_done = sem("qkv_done")
        prod0_done = sem("prod0_done")
        prod1_done = sem("prod1_done")
        scores_ready = sem("scores_ready")
        max_done = sem("max_done")
        shifted = sem("shifted")
        exp_done = sem("exp_done")
        den_done = sem("den_done")
        rden_done = sem("rden_done")
        weighted0_done = sem("weighted0_done")
        weighted1_done = sem("weighted1_done")
        sum_ready = sem("sum_ready")
        attn_done = sem("attn_done")
        attnT_ready = sem("attnT_ready")
        attnT_done = sem("attnT_done")
        oproj_ready = sem("oproj_ready")
        x1_done = sem("x1_done")
        stat2_step = sem("stat2_step")
        norm2_step = sem("norm2_step")
        xhat_done = sem("xhat_done")
        xhatT_ready = sem("xhatT_ready")
        nT_done = sem("nT_done")
        logits_ready = sem("logits_ready")
        lg_done = sem("lg_done")

        lg_in = sem("lg_in")
        route_step = sem("route_step")
        route_exp = sem("route_exp")
        pads_zero = sem("pads_zero")
        sums_ready = sem("sums_ready")
        counts_ready = sem("counts_ready")
        tile_expert_ready = sem("tile_expert_ready")
        onehots_done = sem("onehots_done")
        onehots_used = sem("onehots_used")
        held_ready = sem("held_ready")
        from_done, to_done = sem("from_done"), sem("to_done")
        gathered = sems("gathered")
        scattered = sems("scattered")
        xgT_ready = sem("xgT_ready")
        nTe_done = sem("nTe_done")
        gu_ready = sem("gu_ready")
        silu_done = sem("silu_done")
        hid_done = sem("hid_done")
        hidT_ready = sem("hidT_ready")
        hidT_done = sem("hidT_done")
        down_ready = sem("down_ready")
        y_done = sem("y_done")
        batch_in = sems("batch_in")
        s_gu_ready = sem("s_gu_ready")
        s_silu_done = sem("s_silu_done")
        s_hid_done = sem("s_hid_done")
        s_hidT_ready = sem("s_hidT_ready")
        s_hidT_done = sem("s_hidT_done")
        s_down_ready = sem("s_down_ready")
        mix_step = sem("mix_step")
        out_done = sem("out_done")
        out_stored = sems("out_stored")

        block = ctx.enter_context(nc.Block())

        W_LOADS = 15

        class It:
            def __init__(self, i, r, total):
                self.i, self.r, self.total = i, r, total

            def of(self, off):
                return It(self.i, self.r + off, self.total)

            @property
            def slot(self):
                return self.r % SLOTS

            @property
            def b(self):
                return self.i * SLOTS + self.r

            def times(self, k, add=0):
                return self.i * (SLOTS * k) + (self.r * k + add)

            def round(self, k):
                return self.i * k + (self.r // SLOTS + 1) * k

            @property
            def inside(self):
                return not isinstance(self.i, int) or 0 <= self.b < self.total

        def scores_of(s, e):
            q = qkv[s][:, 0:D].rearrange("p (l h e) -> p l h e", l=N, h=H)[:, :, :, e]
            k = qkv[s][:, D:2 * D].rearrange("p (s h e) -> p h s e", s=N, h=H)[:, :, :, e]
            return (prod[s][:, e, :].rearrange("p (l h s) -> p l h s", l=N, h=H),
                    q.unsqueeze(3).broadcast_to([L, N, H, N]), k.unsqueeze(1).broadcast_to([L, N, H, N]))

        def weighted_of(s, e):
            p = probs[s][:, :].rearrange("p (l h s) -> p s l h", l=N, h=H)
            v = qkv[s][:, 2 * D:3 * D].rearrange("p (s h e) -> p s h e", s=N, h=H)[:, :, :, e]
            return (weighted[s][:, :, :].rearrange("p s (l h e) -> p s l h e", l=N, h=H)[:, :, :, :, e],
                    p, v.unsqueeze(2).broadcast_to([L, N, N, H]))

        spare = {}

        def own_wait(eng, semaphore, value):
            if not isinstance(value, int):
                if eng.engine not in spare:
                    spare[eng.engine] = eng.alloc_register(f"spare{len(spare)}")
                eng.reg_mov(spare[eng.engine], value)
                eng.wait_ge(ident_made, 1)
                value = spare[eng.engine]
            eng.wait_ge(semaphore, value)

        def every(eng, body, begin, first, last, end, total):
            for b in range(begin, first):
                body(It(0, b, total))
            with eng.Fori(0, (last - first) // SLOTS) as i:
                for r in range(first, first + SLOTS):
                    body(It(i, r, total))
            for b in range(last, end):
                body(It(0, b, total))

        def every_iteration(eng, body):
            every(eng, body, -5, 7, 27, B + 3, B)

        def every_pair_column(eng, body):
            every(eng, body, 0, SLOTS, TOP_K * B, TOP_K * B, TOP_K * B)

        def column_of(n, number=1, add=0):
            if isinstance(n.i, int):
                return slice(n.b + add, n.b + add + number)
            return bass.ds(n.times(1, add), number)

        T_FIRST, T_LAST = 6, TILES - 5

        def every_tile(eng, body):
            every(eng, body, -3, T_FIRST, T_LAST, TILES + 2, TILES)

        def every_batch(eng, body):
            every(eng, body, -3, 6, 26, B + 2, B)

        @block.sync
        def _(sp):
            for dst, src in ((wq, t["wq"]), (wkv, t["wkv"]), (wo, t["wo"]),
                             (gamma, t["gamma"]), (beta, t["beta"]), (router, t["router"]),
                             (ws_gu, t["ws_gu"]), (ws_dn, t["ws_dn"]), (bo, t["bo"]),
                             (before, t["before"]), (pair_id, t["pair_id"]), (pad_id, t["pad_id"]),
                             (iota, t["iota"].broadcast_to([L, 128]))):
                sp.dma_start(dst[:, :], src).then_inc(weights_in, 16)
            sp.dma_start(w_gu[:, :, :], t["w_gu"]).then_inc(weights_in, 16)
            sp.dma_start(w_dn[:, :, :], t["w_dn"]).then_inc(weights_in, 16)

            def body(it):
                ld = it.of(5)
                if ld.inside:
                    if it.of(1).inside:
                        own_wait(sp, xcT_ready, it.times(1, 2))
                    sp.dma_start(xin[ld.slot][:, :], t["x"][ld.b]).then_inc(xc_in[ld.slot], 16)
                    sp.dma_start(cin[ld.slot][:, :], t["ctx"][ld.b]).then_inc(xc_in[ld.slot], 16)
                n = it.of(1)
                if n.inside:
                    if it.of(-3).inside:
                        own_wait(sp, x1_done, it.times(1, -2))
                    sp.dma_start(xres[n.slot][:, :], t["x"][n.b]).then_inc(xres_in[n.slot], 16)
                n = it.of(-1)
                if n.inside:
                    sp.wait_ge(x1_done, n.times(1, 1))
                    sp.dma_start(x1_dram[n.b], x1[n.slot][:, :]).then_inc(x1_out[n.slot], 16)
                n = it.of(-2)
                if n.inside:
                    sp.wait_ge(xhat_done, n.times(1, 1))
                    sp.dma_start(xhat_dram.rearrange("(b l) d -> b l d", l=L)[n.b], xhat[n.slot][:, :]).then_inc(xhat_out[n.slot], 16)
                    sp.wait_ge(nT_done, n.times(1, 1))
                    sp.dma_start(nT_dram[n.b], nT[n.slot][:, :]).then_inc(nT_out[n.slot], 16)
                n = it.of(-3)
                if n.inside:
                    sp.wait_ge(lg_done, n.times(1, 1))
                    sp.dma_start(lg_dram[n.b], lg[n.slot][:, :]).then_inc(lg_out[n.slot], 16)

            every_iteration(sp, body)

            for s in range(SLOTS):
                sp.wait_ge(lg_out[s], 16 * (B // SLOTS))
            sp.dma_start(lg_all[:, :, :], lg_dram.rearrange("b l e -> l b e")).then_inc(lg_in, 16)
            for s in range(SLOTS):
                sp.wait_ge(x1_out[s], 16 * (B // SLOTS))
                sp.wait_ge(nT_out[s], 16 * (B // SLOTS))
            for s in range(SLOTS):
                sp.wait_ge(scattered[s], 16 * ((TILES - s + SLOTS - 1) // SLOTS))

            y_of = y_dram[0:PAIRED, :].rearrange("(k b l) d -> k b l d", k=TOP_K, b=B)

            def body(it):
                n = it.of(3)
                if n.inside:
                    s = n.slot
                    if it.of(-1).inside:
                        own_wait(sp, out_done, it.times(1))
                    sp.dma_start(nTf[s][:, :], nT_dram[n.b]).then_inc(batch_in[s], 16)
                    sp.dma_start(x1f[s][:, :], x1_dram[n.b]).then_inc(batch_in[s], 16)
                    for k in range(TOP_K):
                        sp.dma_start(yf[s][k][:, :], y_of[k, n.b]).then_inc(batch_in[s], 16)
                n = it.of(-2)
                if n.inside:
                    sp.wait_ge(out_done, n.times(1, 1))
                    sp.dma_start(t["out"][n.b], out_sb[n.slot][:, :]).then_inc(out_stored[n.slot], 16)

            every_batch(sp, body)
            for s in range(SLOTS):
                sp.wait_ge(out_stored[s], 16 * (B // SLOTS))

        @block.gpsimd
        def _(pool):
            pool.memset(ident[:, :], 0.0).then_inc(const_made, 1)
            pool.memset(minus_half[:, :], -0.5).then_inc(const_made, 1)
            pool.memset(ones[:, :], 1.0).then_inc(const_made, 1)
            pool.memset(all_ones[:, :], 1.0).then_inc(const_made, 1)
            pool.memset(zeros[:, :], 0.0).then_inc(const_made, 1)
            pool.wait_ge(const_made, 5)
            pool.affine_select(out=ident[:, :], in_=ident[:, :], compare_op=ALU.not_equal, fill=1.0, base=0,
                               pattern=[[-1, 128]], channel_multiplier=1).then_inc(ident_made, 1)
            pool.dma_start(bqkv_all[:, :], t["bqkv"].broadcast_to([L, 3 * D])).then_inc(bcast_in, 16)
            for k in range(2):
                pool.dma_start(gates_in[:, k:k + 1], t["g"][:, k:k + 1].broadcast_to([L, 1])).then_inc(bcast_in, 16)

            def body(it):
                if it.inside:
                    pool.wait_ge(exp_done, it.times(1, 1))
                    pool.tensor_tensor(*weighted_of(it.slot, 1), ALU.mult).then_inc(weighted1_done, 1)
                n = it.of(2)
                if n.inside:
                    pool.wait_ge(qkv_done, n.times(1, 1))
                    pool.tensor_tensor(*scores_of(n.slot, 1), ALU.mult).then_inc(prod1_done, 1)
                n = it.of(4)
                if n.inside:
                    s = n.slot
                    own_wait(pool, stat_step, n.times(2, 2))
                    pool.tensor_scalar(vareps[s][:, :], mv[s][:, 1:2], EPS, None, ALU.add).then_inc(norm_step, 1)
                    pool.wait_ge(norm_step, n.times(2, 1))
                    pool.tensor_tensor(rstd[s][:, :], vareps[s][:, :], minus_half[:, :], ALU.pow).then_inc(norm_step, 1)
                n = it.of(-1)
                if n.inside:
                    s = n.slot
                    own_wait(pool, stat2_step, n.times(2, 2))
                    pool.tensor_scalar(vareps2[s][:, :], mv2[s][:, 1:2], 1.0 + EPS, EPS * EPS, ALU.mult, ALU.add)\
                        .then_inc(norm2_step, 1)
                    pool.wait_ge(norm2_step, n.times(2, 1))
                    pool.tensor_tensor(rstd2[s][:, :], vareps2[s][:, :], minus_half[:, :], ALU.pow).then_inc(norm2_step, 1)

            every_iteration(pool, body)

            for s in range(SLOTS):
                pool.wait_ge(xhat_out[s], 16 * (B // SLOTS))

            def tile(it):
                n = it.of(3)
                if n.inside:
                    own_wait(pool, from_done, n.times(1, 1))
                    pool.indirect_dma_start(xg[n.slot][:, :], None, xhat_dram, IndirectOffsetOnAxis(from_now[n.slot][:, :], 0))\
                        .then_inc(gathered[n.slot], 16)
                n = it.of(-2)
                if n.inside:
                    own_wait(pool, y_done, n.times(1, 1))
                    own_wait(pool, to_done, n.times(1, 1))
                    pool.indirect_dma_start(y_dram, IndirectOffsetOnAxis(to_now[n.slot][:, :], 0), y[n.slot][:, :], None)\
                        .then_inc(scattered[n.slot], 16)

            every_tile(pool, tile)

        @block.tensor
        def _(pe):
            pe.wait_ge(weights_in, W_LOADS * 16)
            pe.wait_ge(ident_made, 1)

            def body(it):
                n = it.of(3)
                if n.inside:
                    pe.wait_ge(xc_in[n.slot], n.round(32))
                    pe.wait_ge(xn_done, n.times(1, 1))
                    if n.of(-1).inside:
                        pe.wait_ge(hcT_done, n.times(1))
                    pe.transpose(xcT_ps[:, 0:128], xn[n.slot][:, :], ident[:, :])
                    pe.transpose(xcT_ps[:, 128:256], cin[n.slot][:, :], ident[:, :]).then_inc(xcT_ready, 1)
                n = it.of(-1)
                if n.inside:
                    pe.wait_ge(attn_done, n.times(1, 1))
                    if n.of(-1).inside:
                        pe.wait_ge(attnT_done, n.times(1))
                    pe.transpose(attnT_ps[:, 0:128], attn[n.slot][:, :], ident[:, :]).then_inc(attnT_ready, 1)
                n = it.of(3)
                if n.inside:
                    pe.wait_ge(hcT_done, n.times(1, 1))
                    if n.of(-1).inside:
                        pe.wait_ge(qkv_done, n.times(1))
                    pe.matmul(qkv_ps[:, 0:D], hcT[n.slot][:, 0:L], wq[:, :], start=True, stop=True)
                    pe.matmul(qkv_ps[:, D:3 * D], hcT[n.slot][:, L:2 * L], wkv[:, :], start=True, stop=True).then_inc(qkv_ready, 1)
                n = it.of(-1)
                if n.inside:
                    if n.of(-1).inside:
                        pe.wait_ge(x1_done, n.times(1))
                    pe.matmul(oproj_ps[:, 0:D], ones[:, :], bo[:, :], start=True, stop=False)
                    pe.wait_ge(attnT_done, n.times(1, 1))
                    pe.matmul(oproj_ps[:, 0:D], attnT[n.slot][:, :], wo[:, :], start=False, stop=True).then_inc(oproj_ready, 1)
                if it.inside:
                    pe.wait_ge(weighted0_done, it.times(1, 1))
                    pe.wait_ge(weighted1_done, it.times(1, 1))
                    if it.of(-1).inside:
                        pe.wait_ge(attn_done, it.times(1))
                    for k in range(N):
                        last = pe.matmul(sum_ps[:, 0:D], ident[:, :], weighted[it.slot][:, k, :], start=(k == 0), stop=(k == N - 1))
                    last.then_inc(sum_ready, 1)
                n = it.of(-2)
                if n.inside:
                    pe.wait_ge(xhat_done, n.times(1, 1))
                    if n.of(-1).inside:
                        pe.wait_ge(lg_done, n.times(1))
                    pe.transpose(tail_ps[:, 0:128], xhat[n.slot][:, :], ident[:, :]).then_inc(xhatT_ready, 1)
                n = it.of(2)
                if n.inside:
                    pe.wait_ge(prod0_done, n.times(1, 1))
                    pe.wait_ge(prod1_done, n.times(1, 1))
                    if n.of(-2).inside:
                        pe.wait_ge(shifted, n.times(1, -1))
                    pe.matmul(score_ps[n.r % 2][:, :], ident[:, :], prod[n.slot][:, 0, :], start=True, stop=False)
                    pe.matmul(score_ps[n.r % 2][:, :], ident[:, :], prod[n.slot][:, 1, :], start=False, stop=True)\
                        .then_inc(scores_ready, 1)
                n = it.of(-2)
                if n.inside:
                    pe.wait_ge(nT_done, n.times(1, 1))
                    pe.matmul(tail_ps[:, 0:EXPERTS], nT[n.slot][:, :], router[:, :], start=True, stop=True)\
                        .then_inc(logits_ready, 1)

            every_iteration(pe, body)

            pe.wait_ge(const_made, 5)
            pe.wait_ge(sums_ready, 1)
            sums = count[1][:, PAD + B - 1, :]
            pe.matmul(count_ps[:, 0:EXPERTS], before[:, :], sums, start=True, stop=True)
            pe.matmul(count_ps[:, EXPERTS:2 * EXPERTS], all_ones[:, :], sums, start=True, stop=True).then_inc(counts_ready, 1)

            pe.matmul(held_ps[:, 0:TILES], all_ones[:, :], zeros[:, :], start=True, stop=False)

            def pair_column(it):
                pe.wait_ge(onehots_done, it.times(1, 1))
                pe.matmul(held_ps[:, 0:TILES], onehot_in[it.slot][:, :], onehot_tile[it.slot][:, :],
                          start=False, stop=False).then_inc(onehots_used, 1)

            every_pair_column(pe, pair_column)
            pe.matmul(held_ps[:, 0:TILES], all_ones[:, :], zeros[:, :], start=False, stop=True).then_inc(held_ready, 1)

            w_gu_flat = w_gu[:, :, :].rearrange("d e f -> d (e f)")
            w_dn_flat = w_dn[:, :, :].rearrange("f c d -> f (c d)")
            front = (0, [pe.alloc_register(f"front_expert{k}") for k in range(T_FIRST)])
            looped = (T_FIRST - 2, [pe.alloc_register(f"expert{k}") for k in range(SLOTS + 2)])
            behind_loop = (T_LAST - 2, [pe.alloc_register(f"last_expert{k}") for k in range(TILES - T_LAST + 2)])

            def expert_of(n, held_in):
                first, registers = held_in
                return bass.RuntimeValue.of_register_unchecked(registers[n.r - first], min_val=0, max_val=EXPERTS - 1)

            def tile(it):
                experts = looped if not isinstance(it.i, int) else front if it.r < T_FIRST else behind_loop
                if it.r in (-3, T_FIRST, T_LAST):
                    first, registers = experts
                    if it.r == -3:
                        pe.wait_ge(tile_expert_ready, 1)
                    n = it.of(first - it.r)
                    pe.load(registers, tile_expert[0:1, column_of(n, len(registers))])
                n = it
                if n.inside:
                    e = expert_of(n, experts)
                    k = n.slot % 2
                    pe.wait_ge(nTe_done, n.times(1, 1))
                    if n.of(-2).inside:
                        pe.wait_ge(hid_done, n.times(1, -1))
                    pe.matmul(pairs[k][:, 0, 0:F], nTe[k][:, :], w_gu_flat[:, bass.ds(e * (2 * F), F)], start=True, stop=True)
                    pe.matmul(pairs[k][:, 1, 0:F], nTe[k][:, :], w_gu_flat[:, bass.ds(e * (2 * F) + F, F)], start=True, stop=True)\
                        .then_inc(gu_ready, 1)
                n = it.of(1)
                if n.inside:
                    pe.wait_ge(gathered[n.slot], n.round(16))
                    if n.of(-1).inside:
                        pe.wait_ge(nTe_done, n.times(1))
                    pe.transpose(xgT_ps[:, 0:128], xg[n.slot][:, :], ident[:, :]).then_inc(xgT_ready, 1)
                n = it.of(-1)
                if n.inside:
                    k = n.slot % 2
                    pe.wait_ge(hid_done, n.times(1, 1))
                    if n.of(-2).inside:
                        pe.wait_ge(hidT_done, n.times(1, -1))
                    for c in range(FC):
                        last = pe.transpose(hidT_ps[k][:, c * 128:(c + 1) * 128], hid[k][:, c * 128:(c + 1) * 128], ident[:, :])
                    last.then_inc(hidT_ready, 1)
                n = it.of(-2)
                if n.inside:
                    e = expert_of(n, experts)
                    k = n.slot % 2
                    pe.wait_ge(hidT_done, n.times(1, 1))
                    if n.of(-1).inside:
                        pe.wait_ge(y_done, n.times(1))
                    for c in range(FC):
                        last = pe.matmul(down_ps[:, 0:D], hidT[k][:, c * 128:(c + 1) * 128],
                                         w_dn_flat[:, bass.ds(e * (FC * D) + c * D, D)], start=(c == 0), stop=(c == FC - 1))
                    last.then_inc(down_ready, 1)

            pe.wait_ge(from_done, 1)
            every_tile(pe, tile)

            pe.wait_ge(y_done, TILES)

            def batch(it):
                n = it
                if n.inside:
                    k = n.slot % 2
                    pe.wait_ge(batch_in[n.slot], n.round(16 * (2 + TOP_K)))
                    if n.of(-2).inside:
                        pe.wait_ge(s_hid_done, n.times(1, -1))
                    pe.matmul(pairs[k][:, 0, 0:FS], nTf[n.slot][:, :], ws_gu[:, 0:FS], start=True, stop=True)
                    pe.matmul(pairs[k][:, 1, 0:FS], nTf[n.slot][:, :], ws_gu[:, FS:2 * FS], start=True, stop=True)\
                        .then_inc(s_gu_ready, 1)
                n = it.of(-1)
                if n.inside:
                    k = n.slot % 2
                    pe.wait_ge(s_hid_done, n.times(1, 1))
                    if n.of(-2).inside:
                        pe.wait_ge(s_hidT_done, n.times(1, -1))
                    pe.transpose(hidT_ps[k][:, 0:FS], hid[k][:, 0:FS], ident[:, :]).then_inc(s_hidT_ready, 1)
                n = it.of(-2)
                if n.inside:
                    k = n.slot % 2
                    pe.wait_ge(s_hidT_done, n.times(1, 1))
                    if n.of(-1).inside:
                        pe.wait_ge(out_done, n.times(1))
                    pe.matmul(down_ps[:, 0:D], hidT[k][:, 0:FS], ws_dn[:, :], start=True, stop=True).then_inc(s_down_ready, 1)

            every_batch(pe, batch)

        @block.scalar
        def _(act):
            act.wait_ge(bcast_in, 48)
            act.activation(gates[:, :], gates_in[:, :], ACT.Tanh).then_inc(gates_done, 1)
            act.wait_ge(weights_in, W_LOADS * 16)

            def body(it):
                n = it.of(3)
                if n.inside:
                    act.wait_ge(xcT_ready, n.times(1, 1))
                    act.activation(hcT[n.slot][:, :], xcT_ps[:, 0:256], ACT.Copy).then_inc(hcT_done, 1)
                n = it.of(-1)
                if n.inside:
                    act.wait_ge(attnT_ready, n.times(1, 1))
                    act.activation(attnT[n.slot][:, :], attnT_ps[:, 0:128], ACT.Copy).then_inc(attnT_done, 1)
                n = it.of(1)
                if n.inside:
                    act.wait_ge(shifted, n.times(1, 1))
                    act.activation(probs[n.slot][:, :], probs[n.slot][:, :], ACT.Exp, scale=SM_SCALE).then_inc(exp_done, 1)
                n = it.of(-2)
                if n.inside:
                    act.wait_ge(xhatT_ready, n.times(1, 1))
                    if n.of(-4).inside:
                        act.wait_ge(nT_out[n.slot], n.of(-4).round(16))
                    act.activation(nT[n.slot][:, :], tail_ps[:, 0:128], ACT.Identity, bias=beta[:, 0:1], scale=gamma[:, 0:1])\
                        .then_inc(nT_done, 1)

            every_iteration(act, body)

            act.wait_ge(route_step, 2)
            act.activation(rt[1][:, :, :], rt[0][:, :, :], ACT.Exp).then_inc(route_exp, 1)
            act.wait_ge(route_step, ROUTE_GATE)
            act.activation(rs[3][:, :], rs[2][:, :], ACT.Exp).then_inc(route_exp, 1)

            def tile(it):
                n = it.of(1)
                if n.inside:
                    act.wait_ge(xgT_ready, n.times(1, 1))
                    act.activation(nTe[n.slot % 2][:, :], xgT_ps[:, 0:128], ACT.Identity, bias=beta[:, 0:1], scale=gamma[:, 0:1])\
                        .then_inc(nTe_done, 1)
                n = it
                if n.inside:
                    k = n.slot % 2
                    act.wait_ge(gu_ready, n.times(1, 1))
                    act.activation(silu[k][:, :], pairs[k][:, 0, 0:F], ACT.Silu).then_inc(silu_done, 1)
                n = it.of(-1)
                if n.inside:
                    k = n.slot % 2
                    act.wait_ge(hidT_ready, n.times(1, 1))
                    act.activation(hidT[k][:, :], hidT_ps[k][:, 0:F], ACT.Copy).then_inc(hidT_done, 1)

            every_tile(act, tile)

            def batch(it):
                n = it
                if n.inside:
                    k = n.slot % 2
                    act.wait_ge(s_gu_ready, n.times(1, 1))
                    act.activation(silu[k][:, 0:FS], pairs[k][:, 0, 0:FS], ACT.Silu).then_inc(s_silu_done, 1)
                n = it.of(-1)
                if n.inside:
                    k = n.slot % 2
                    act.wait_ge(s_hidT_ready, n.times(1, 1))
                    act.activation(hidT[k][:, 0:FS], hidT_ps[k][:, 0:FS], ACT.Copy).then_inc(s_hidT_done, 1)

            every_batch(act, batch)

        @block.vector
        def _(dve):
            def heads(ap):
                return ap.rearrange("p (n e) -> p n e", e=E2)

            def by_s(ap):
                return ap.rearrange("p (n s) -> p n s", s=N)

            def body(it):
                n = it.of(3)
                if n.inside:
                    s = n.slot
                    own_wait(dve, norm_step, n.times(2, 2))
                    dve.tensor_scalar(xn[s][:, :], xin[s][:, :], mv[s][:, 0:1], rstd[s][:, 0:1],
                                      ALU.subtract, ALU.mult).then_inc(xn_done, 1)
                n = it.of(-3)
                if n.inside:
                    s = n.slot
                    dve.wait_ge(logits_ready, n.times(1, 1))
                    if n.of(-4).inside:
                        dve.wait_ge(lg_out[s], n.of(-4).round(16))
                    dve.tensor_copy(lg[s][:, :], tail_ps[:, 0:EXPERTS]).then_inc(lg_done, 1)
                n = it.of(2)
                if n.inside:
                    dve.wait_ge(qkv_ready, n.times(1, 1))
                    dve.tensor_tensor(qkv[n.slot][:, :], qkv_ps[:, 0:3 * D], bqkv_all[:, :], ALU.add).then_inc(qkv_done, 1)
                n = it.of(-1)
                if n.inside:
                    s = n.slot
                    dve.wait_ge(sum_ready, n.times(1, 1))
                    dve.wait_ge(rden_done, n.times(1, 1))
                    dve.tensor_tensor(heads(attn[s][:, :]), heads(sum_ps[:, 0:D]), rden[s][:, :].unsqueeze(2).broadcast_to([L, NH, E2]),
                                      ALU.mult).then_inc(attn_done, 1)
                if it.inside:
                    dve.wait_ge(exp_done, it.times(1, 1))
                    dve.tensor_tensor(*weighted_of(it.slot, 0), ALU.mult).then_inc(weighted0_done, 1)
                n = it.of(2)
                if n.inside:
                    dve.wait_ge(qkv_done, n.times(1, 1))
                    dve.tensor_tensor(*scores_of(n.slot, 0), ALU.mult).then_inc(prod0_done, 1)
                n = it.of(-2)
                if n.inside:
                    s = n.slot
                    own_wait(dve, norm2_step, n.times(2, 2))
                    if n.of(-4).inside:
                        own_wait(dve, xhat_out[s], n.of(-4).round(16))
                    dve.tensor_scalar(xhat[s][:, :], x1[s][:, :], mv2[s][:, 0:1], rstd2[s][:, 0:1],
                                      ALU.subtract, ALU.mult).then_inc(xhat_done, 1)
                n = it.of(4)
                if n.inside:
                    s = n.slot
                    dve.wait_ge(xc_in[s], n.round(32))
                    dve.bn_stats(stats[s][:, :], xin[s][:, :]).then_inc(stat_step, 1)
                n = it.of(1)
                if n.inside:
                    s = n.slot
                    dve.wait_ge(scores_ready, n.times(1, 1))
                    dve.tensor_reduce(smax[s][:, :], by_s(score_ps[n.r % 2][:, :]), AX.X, ALU.max).then_inc(max_done, 1)
                n = it.of(4)
                if n.inside:
                    own_wait(dve, stat_step, n.times(2, 1))
                    dve.bn_aggr(mv[n.slot][:, :], stats[n.slot][:, :]).then_inc(stat_step, 1)
                n = it.of(1)
                if n.inside:
                    s = n.slot
                    dve.wait_ge(max_done, n.times(1, 1))
                    dve.tensor_tensor(by_s(probs[s][:, :]), by_s(score_ps[n.r % 2][:, :]), smax[s][:, :].unsqueeze(2).broadcast_to([L, NH, N]),
                                      ALU.subtract).then_inc(shifted, 1)
                n = it.of(-1)
                if n.inside:
                    s = n.slot
                    dve.wait_ge(oproj_ready, n.times(1, 1))
                    dve.wait_ge(xres_in[s], n.round(16))
                    if n.of(-4).inside:
                        dve.wait_ge(x1_out[s], n.of(-4).round(16))
                    dve.scalar_tensor_tensor(x1[s][:, :], oproj_ps[:, 0:D], gates[:, 0:1], xres[s][:, :], ALU.mult, ALU.add)\
                        .then_inc(x1_done, 1)
                    dve.wait_ge(x1_done, n.times(1, 1))
                    dve.bn_stats(stats2[s][:, :], x1[s][:, :]).then_inc(stat2_step, 1)
                if it.inside:
                    s = it.slot
                    dve.tensor_reduce(den[s][:, :], by_s(probs[s][:, :]), AX.X, ALU.add).then_inc(den_done, 1)
                n = it.of(-1)
                if n.inside:
                    own_wait(dve, stat2_step, n.times(2, 1))
                    dve.bn_aggr(mv2[n.slot][:, :], stats2[n.slot][:, :]).then_inc(stat2_step, 1)
                if it.inside:
                    s = it.slot
                    dve.wait_ge(den_done, it.times(1, 1))
                    dve.reciprocal(rden[s][:, :], den[s][:, :]).then_inc(rden_done, 1)

            dve.wait_ge(gates_done, 1)
            dve.wait_ge(bcast_in, 48)
            every_iteration(dve, body)

            steps = [0]

            def step(ins):
                steps[0] += 1
                ins.then_inc(route_step, 1)
                dve.wait_ge(route_step, steps[0])

            def over_e(a):
                return a.unsqueeze(2).broadcast_to([L, B, EXPERTS])

            for e in range(EXPERTS):
                last = dve.memset(iota_e[:, e:e + 1], float(e - EXPERTS))
            for buffer in (count[0][:, 0:PAD, :], count[1][:, 0:PAD, :], tiles_of[0][:, 0:PAD_E], tiles_of[1][:, 0:PAD_E]):
                dve.memset(buffer, 0.0).then_inc(pads_zero, 1)
            dve.wait_ge(pads_zero, 4)
            by_expert = iota_e[:, :].unsqueeze(1).broadcast_to([L, B, EXPERTS])
            dve.wait_ge(lg_in, 16)
            step(dve.tensor_reduce(rs[0][:, :], lg_all[:, :, :], AX.X, ALU.max))
            step(dve.tensor_tensor(rt[0][:, :, :], lg_all[:, :, :], over_e(rs[0][:, :]), ALU.subtract))
            dve.wait_ge(route_exp, 1)
            step(dve.tensor_reduce(rs[0][:, :], rt[1][:, :, :], AX.X, ALU.add))
            step(dve.reciprocal(rs[1][:, :], rs[0][:, :]))
            step(dve.tensor_tensor(rt[0][:, :, :], rt[1][:, :, :], over_e(rs[1][:, :]), ALU.mult))

            def top(p, onehot, value, scratch, index):
                step(dve.tensor_reduce(value, p, AX.X, ALU.max))
                step(dve.tensor_tensor(scratch, p, over_e(value), ALU.is_equal))
                step(dve.tensor_tensor(scratch, scratch, by_expert, ALU.mult))
                step(dve.tensor_reduce(index, scratch, AX.X, ALU.min))
                step(dve.tensor_tensor(onehot, by_expert, over_e(index), ALU.is_equal))

            top(rt[0][:, :, :], rt[2][:, :, :], rs[0][:, :], rt[1][:, :, :], rs[2][:, :])
            step(dve.scalar_tensor_tensor(rt[3][:, :, :], rt[2][:, :, :], -2.0, rt[0][:, :, :], ALU.mult, ALU.add))
            top(rt[3][:, :, :], rt[0][:, :, :], rs[1][:, :], rt[1][:, :, :], rs[2][:, :])
            step(dve.tensor_tensor(rs[2][:, :], rs[1][:, :], rs[0][:, :], ALU.subtract))
            assert steps[0] == ROUTE_GATE
            dve.wait_ge(route_exp, 2)
            step(dve.tensor_scalar(rs[0][:, :], rs[3][:, :], 1.0, None, ALU.add))
            step(dve.reciprocal(rs[1][:, :], rs[0][:, :]))
            step(dve.tensor_tensor(rs[2][:, :], rs[1][:, :], rs[3][:, :], ALU.mult))
            dve.tensor_scalar(pair_gate[:, 0:B], rs[1][:, :], gates[:, 1:2], None, ALU.mult)
            step(dve.tensor_scalar(pair_gate[:, B:2 * B], rs[2][:, :], gates[:, 1:2], None, ALU.mult))

            first, second = rt[2], rt[0]
            step(dve.tensor_tensor(count[0][:, PAD:, :], first[:, :, :], second[:, :, :], ALU.add))
            for k in range(5):
                a, b = count[k % 2], count[(k + 1) % 2]
                ins = dve.tensor_tensor(b[:, PAD:, :], a[:, PAD:, :], a[:, PAD - (1 << k):PAD + B - (1 << k), :], ALU.add)
                if k < 4:
                    step(ins)
                else:
                    ins.then_inc(sums_ready, 1)
            dve.wait_ge(sums_ready, 1)
            dve.wait_ge(counts_ready, 1)
            dve.wait_ge(weights_in, W_LOADS * 16)
            step(dve.tensor_scalar(count_tiles[:, :], count_ps[:, EXPERTS:2 * EXPERTS], 1.0 / 128, None, ALU.mult))
            step(dve.tensor_tensor(count_over[:, :, :], count_tiles[:, :].unsqueeze(2).broadcast_to([L, EXPERTS, B]),
                                   iota[:, 0:B].unsqueeze(1).broadcast_to([L, EXPERTS, B]), ALU.is_gt))
            step(dve.tensor_reduce(tiles_of[0][:, PAD_E:], count_over[:, :, :], AX.X, ALU.add))
            for k in range(3):
                a, b = tiles_of[k % 2], tiles_of[(k + 1) % 2]
                step(dve.tensor_tensor(b[:, PAD_E:], a[:, PAD_E:], a[:, PAD_E - (1 << k):PAD_E + EXPERTS - (1 << k)], ALU.add))
            tiles_up_to = tiles_of[1]
            step(dve.scalar_tensor_tensor(first_row[:, :], tiles_up_to[:, PAD_E - 1:PAD_E + EXPERTS - 1], 128.0, count_ps[:, 0:EXPERTS],
                                          ALU.mult, ALU.add))
            step(dve.tensor_tensor(rt[1][:, :, :], count[1][:, PAD - 1:PAD + B - 1, :],
                                   first_row[:, :].unsqueeze(1).broadcast_to([L, B, EXPERTS]), ALU.add))
            for k, onehot in enumerate((first, second)):
                step(dve.tensor_tensor(rt[3][:, :, :], onehot[:, :, :], rt[1][:, :, :], ALU.mult))
                step(dve.tensor_reduce(row[:, k, :], rt[3][:, :, :], AX.X, ALU.add))
            rows = row[:, :, :].rearrange("l k b -> l (k b)")
            step(dve.tensor_scalar(row_tile[:, :], rows, 1.0 / 128, -63.5 / 128, ALU.mult, ALU.add))
            step(dve.tensor_scalar(row_in_tile[:, :], row_tile[:, :], ROUND_UP, None, ALU.add))
            step(dve.tensor_scalar(row_tile[:, :], row_in_tile[:, :], -ROUND_UP, None, ALU.add))
            step(dve.scalar_tensor_tensor(row_in_tile[:, :], row_tile[:, :], -128.0, rows, ALU.mult, ALU.add))

            def pair_column(it):
                s = it.slot
                column = column_of(it)
                if it.of(-4).inside:
                    own_wait(dve, onehots_used, it.times(1, -3))
                dve.tensor_scalar(onehot_in[s][:, :], iota[:, :], row_in_tile[:, column], None, ALU.is_equal)
                dve.tensor_scalar(onehot_tile[s][:, :], iota[:, 0:TILES], row_tile[:, column], pair_id[:, column],
                                  ALU.is_equal, ALU.mult).then_inc(onehots_done, 1)

            every_pair_column(dve, pair_column)

            step(dve.tensor_tensor(behind[:, :, :], tiles_up_to[0:1, PAD_E:].unsqueeze(1).broadcast_to([1, TILES, EXPERTS]),
                                   iota[0:1, 0:TILES].unsqueeze(2).broadcast_to([1, TILES, EXPERTS]), ALU.is_le))
            step(dve.tensor_reduce(tile_expert_f[:, :], behind[:, :, :], AX.X, ALU.add))
            step(dve.tensor_scalar(tile_expert_f[:, :], tile_expert_f[:, :], EXPERTS - 1.0, None, ALU.min))
            dve.tensor_copy(tile_expert[:, :], tile_expert_f[:, :]).then_inc(tile_expert_ready, 1)
            dve.wait_ge(held_ready, 1)
            pair, second_off, pad_to, src, dst = (h[:, :] for h in held)
            step(dve.tensor_scalar(pair, held_ps[:, 0:TILES], -1.0, None, ALU.add))
            step(dve.tensor_scalar(second_off, pair, float(TOKENS), -float(TOKENS), ALU.is_ge, ALU.mult))
            step(dve.scalar_tensor_tensor(pad_to, pair, 0.0, pad_id[:, :], ALU.is_lt, ALU.mult))
            step(dve.tensor_tensor(src, pair, second_off, ALU.add))
            step(dve.tensor_tensor(dst, pair, pad_to, ALU.add))
            step(dve.tensor_scalar(src, src, 0.0, TOKENS - 1.0, ALU.max, ALU.min))
            step(dve.tensor_scalar(dst, dst, 0.0, Y_ROWS - 1.0, ALU.max, ALU.min))
            step(dve.tensor_copy(from_row[:, :], src))
            step(dve.tensor_copy(to_row[:, :], dst))

            def tile(it):
                n = it.of(3)
                if n.inside:
                    dve.tensor_copy(from_now[n.slot][:, :], from_row[:, column_of(n)]).then_inc(from_done, 1)
                n = it.of(-2)
                if n.inside:
                    s = n.slot
                    if n.of(-4).inside:
                        dve.wait_ge(scattered[s], n.of(-4).round(16))
                    dve.tensor_copy(to_now[s][:, :], to_row[:, column_of(n)]).then_inc(to_done, 1)
                    dve.wait_ge(down_ready, n.times(1, 1))
                    dve.tensor_copy(y[s][:, :], down_ps[:, 0:D]).then_inc(y_done, 1)
                n = it
                if n.inside:
                    k = n.slot % 2
                    dve.wait_ge(silu_done, n.times(1, 1))
                    dve.tensor_tensor(hid[k][:, :], pairs[k][:, 1, 0:F], silu[k][:, :], ALU.mult).then_inc(hid_done, 1)

            every_tile(dve, tile)

            def batch(it):
                n = it
                if n.inside:
                    s, k = n.slot, n.slot % 2
                    gate = [column_of(n, add=j * B) for j in range(TOP_K)]
                    dve.wait_ge(batch_in[s], n.round(16 * (2 + TOP_K)))
                    dve.scalar_tensor_tensor(x1f[s][:, :], yf[s][0][:, :], pair_gate[:, gate[0]], x1f[s][:, :],
                                             ALU.mult, ALU.add).then_inc(mix_step, 1)
                    dve.wait_ge(s_silu_done, n.times(1, 1))
                    dve.tensor_tensor(hid[k][:, 0:FS], pairs[k][:, 1, 0:FS], silu[k][:, 0:FS], ALU.mult).then_inc(s_hid_done, 1)
                    own_wait(dve, mix_step, n.times(2, 1))
                    dve.scalar_tensor_tensor(x1f[s][:, :], yf[s][1][:, :], pair_gate[:, gate[1]], x1f[s][:, :],
                                             ALU.mult, ALU.add).then_inc(mix_step, 1)
                n = it.of(-2)
                if n.inside:
                    s = n.slot
                    own_wait(dve, s_down_ready, n.times(1, 1))
                    own_wait(dve, mix_step, n.times(2, 2))
                    if n.of(-4).inside:
                        own_wait(dve, out_stored[s], n.of(-4).round(16))
                    dve.scalar_tensor_tensor(out_sb[s][:, :], down_ps[:, 0:D], gates[:, 1:2], x1f[s][:, :],
                                             ALU.mult, ALU.add).then_inc(out_done, 1)

            every_batch(dve, batch)


ROUTE_GATE = 17


def kernel(**inputs):
    import concourse.bacc as bacc
    from concourse.bass_utils import run_bass_kernel_spmd

    a = {k: np.asarray(v) for k, v in inputs.items()}
    gu = a["L0_ffn_gate_up_w"]
    arrays = {
        "x": a["x"], "ctx": a["ctx_1024"],
        "g": np.concatenate([a["g_xattn"], a["g_ffn"]]).reshape(1, 2),
        "wq": a["L0_xattn_Wq"].T, "wkv": np.concatenate([a["L0_xattn_Wk"], a["L0_xattn_Wv"]]).T,
        "bqkv": np.concatenate([a["L0_xattn_bq"], a["L0_xattn_bk"], a["L0_xattn_bv"]]).reshape(1, 3 * D),
        "wo": a["L0_xattn_Wo"].T, "bo": a["L0_xattn_bo"].reshape(1, D),
        "gamma": a["L0_ffn_ln_gamma"].reshape(D, 1), "beta": a["L0_ffn_ln_beta"].reshape(D, 1),
        "router": a["L0_ffn_router_w"].T,
        "w_gu": gu.transpose(2, 0, 1),
        "w_dn": a["L0_ffn_down_w"].transpose(0, 2, 1).reshape(EXPERTS, FC, 128, D).transpose(2, 0, 1, 3).reshape(128, EXPERTS * FC, D),
        "before": np.triu(np.ones((128, 128), np.float32), 1), "iota": np.arange(128, dtype=np.float32).reshape(1, 128),
        "pair_id": (np.arange(TOP_K * B)[None, :] * L + np.arange(L)[:, None] + 1).astype(np.float32),
        "pad_id": (PAIRED + np.arange(TILES)[None, :] * 128 + np.arange(128)[:, None] + 1).astype(np.float32),
        "ws_gu": a["L0_ffn_shared_gate_up_w"].T, "ws_dn": a["L0_ffn_shared_down_w"].T,
    }
    nc = bacc.Bacc("TRN2", target_bir_lowering=False, num_devices=1)
    fed, t = {}, {}
    for name, v in arrays.items():
        v = np.ascontiguousarray(v)
        fed[f"in_{name}"] = v
        t[name] = nc.dram_tensor(f"in_{name}", v.shape, mybir.dt.from_np(v.dtype), kind="ExternalInput").ap()
    t["out"] = nc.dram_tensor("out", [B, L, D], FP32, kind="ExternalOutput").ap()
    attention_then_moe(nc, t)
    r = run_bass_kernel_spmd(nc, [fed], core_ids=[0])
    return r.results[0]["out"]
```

```python
import numpy as np

import concourse.bass as bass
from concourse import mybir
from concourse.bass import IndirectOffsetOnAxis
from contextlib import ExitStack

FP32 = mybir.dt.float32
BF16 = mybir.dt.bfloat16
INT32 = mybir.dt.int32
ALU = mybir.AluOpType
ACT = mybir.ActivationFunctionType
AX = mybir.AxisListType

B = 32
L = 128
D = 128
N, H, E2 = 8, 8, 2
NH = N * H
PAIRS = N * H * N
EPS = 1e-5
SM_SCALE = 1.0 / np.sqrt(E2)
EXPERTS = 8
F = 384
FS = 128
FC = F // 128
TOKENS = B * L
TOP_K = 2
PAIRED = TOP_K * TOKENS
TILES = PAIRED // 128 + EXPERTS - 1
Y_ROWS = PAIRED + TILES * 128
SLOTS = 4
GROUP, BUFFERS = 2, 4
ROUND_UP = 1.5 * 2.0 ** 23


def attention_then_moe(nc, t):
    ctx = ExitStack()
    with ctx:
        def sb(name, shape, dt=FP32):
            return ctx.enter_context(nc.sbuf_tensor(name, shape, dt))

        def ps(name, shape, dt=FP32):
            return ctx.enter_context(nc.psum_tensor(name, shape, dt))

        def sem(name):
            return ctx.enter_context(nc.semaphore(name))

        def sems(name):
            return [sem(f"{name}{i}") for i in range(SLOTS)]

        xhat_dram = nc.dram_tensor("xhat_dram", [TOKENS, D], FP32).ap()
        y_dram = nc.dram_tensor("y_dram", [Y_ROWS, D], FP32).ap()

        wq, wkv, wo = sb("wq_sb", [D, D]), sb("wkv_sb", [D, 2 * D]), sb("wo_sb", [D, D])
        bqkv_all = sb("bqkv_all", [L, 3 * D])
        bo = sb("bo_sb", [1, D])
        ones = sb("ones", [1, L])
        gamma, beta = sb("gamma_sb", [D, 1]), sb("beta_sb", [D, 1])
        router = sb("router_sb", [D, EXPERTS])
        w_gu = sb("w_gu", [D, EXPERTS, 2 * F])
        w_dn = sb("w_dn", [128, EXPERTS * FC, D])
        ws_gu = sb("ws_gu", [D, 2 * FS])
        ws_dn = sb("ws_dn", [FS, D])
        gates_in = sb("gates_in", [L, 2])
        gates = sb("gates", [L, 2])
        ident = sb("ident", [128, 128])
        minus_half = sb("minus_half", [L, 1])

        def slots(name, shape):
            return [sb(f"{name}{i}", shape) for i in range(SLOTS)]

        x_all = sb("x_all", [L, B * D])
        cin = slots("cin", [L, D])
        stats, mv = slots("stats", [L, 6]), slots("mv", [L, 2])
        vareps, rstd, shift = slots("vareps", [L, 1]), slots("rstd", [L, 1]), slots("shift", [L, 1])
        xn = slots("xn", [L, D])
        hcT = slots("hcT", [D, 2 * L])
        qkv = slots("qkv", [L, 3 * D])
        prod = slots("prod", [L, E2, PAIRS])
        smax = slots("smax", [L, NH])
        probs = slots("probs", [L, PAIRS])
        weighted = slots("weighted", [L, N, D])
        den, rden = slots("den", [L, NH]), slots("rden", [L, NH])
        attn, attnT = slots("attn", [L, D]), slots("attnT", [D, L])
        stats2, mv2 = slots("stats2_", [L, 6]), slots("mv2_", [L, 2])
        vareps2, rstd2, shift2 = slots("vareps2_", [L, 1]), slots("rstd2_", [L, 1]), slots("shift2_", [L, 1])
        xhat = slots("xhat", [L, D])
        nT = slots("nT", [D, L])
        nT_all = sb("nT_all", [D, B * L])

        lg_all = sb("lg_all", [L, B, EXPERTS])
        pair_gate = sb("pair_gate", [L, TOP_K * B])
        iota = sb("iota", [L, 128])
        before = sb("before", [128, 128])
        all_ones = sb("all_ones", [128, 128])
        column_no, token_no = sb("column_no", [L, TOP_K * B]), sb("token_no", [L, 1])
        pad_id = sb("pad_id", [L, TILES])
        PAD, PAD_E = B // 2, EXPERTS // 2
        count = [sb(f"count{i}", [L, PAD + B, EXPERTS]) for i in range(2)]
        tiles_of = [sb(f"tiles_of{i}", [L, PAD_E + EXPERTS]) for i in range(2)]
        count_over = sb("count_over", [L, EXPERTS, B])
        count_tiles = sb("count_tiles", [L, EXPERTS])
        first_row = sb("first_row", [L, EXPERTS])
        row = sb("row", [L, TOP_K, B])
        row_tile, row_in_tile = sb("row_tile", [L, TOP_K * B]), sb("row_in_tile", [L, TOP_K * B])
        COLUMNS, COLUMN_BUFFERS = 4, 4
        onehot_in = [sb(f"onehot_in{i}", [L, COLUMNS, 128], BF16) for i in range(COLUMN_BUFFERS)]
        onehot_tile = [sb(f"onehot_tile{i}", [L, COLUMNS, TILES], BF16) for i in range(COLUMN_BUFFERS)]
        token_tile = [sb(f"token_tile{i}", [L, COLUMNS, TILES], BF16) for i in range(COLUMN_BUFFERS)]
        column_tile = [sb(f"column_tile{i}", [L, COLUMNS, TILES], BF16) for i in range(COLUMN_BUFFERS)]
        zeros = sb("zeros", [128, 2 * TILES], BF16)
        ones_bf = sb("ones_bf", [128, 128], BF16)
        behind = sb("behind", [1, TILES, EXPERTS])
        tile_expert_f, tile_expert = sb("tile_expert_f", [1, TILES]), sb("tile_expert", [1, TILES], INT32)
        held = [sb(f"held{i}", [128, TILES]) for i in range(5)]
        from_row, to_row = sb("from_row", [128, TILES], INT32), sb("to_row", [128, TILES], INT32)
        rt = [sb(f"rt{i}", [L, B, EXPERTS]) for i in range(4)]
        rs = [sb(f"rs{i}", [L, B]) for i in range(4)]
        iota_e = sb("iota_e", [L, EXPERTS])

        from_now = [sb(f"from_now{i}", [128, 1], INT32) for i in range(SLOTS)]
        to_now = [sb(f"to_now{i}", [128, 1], INT32) for i in range(SLOTS)]
        xg = [sb(f"xg{i}", [128, D]) for i in range(SLOTS)]
        y = [sb(f"y{i}", [128, D]) for i in range(SLOTS)]
        nTe = [sb(f"nTe{i}", [D, L]) for i in range(2)]
        silu = [sb(f"silu{i}", [L, F]) for i in range(2)]
        hid = [sb(f"hid{i}", [L, F]) for i in range(2)]
        hidT = [sb(f"hidT{i}", [128, F]) for i in range(2)]
        nTf = [sb(f"nTf{i}", [D, L]) for i in range(SLOTS)]
        yf = [[sb(f"yf{i}_{k}", [L, GROUP, D]) for k in range(TOP_K)] for i in range(BUFFERS)]
        gated = [sb(f"gated{i}", [L, D]) for i in range(SLOTS)]
        mix = [sb(f"mix{i}", [L, D]) for i in range(SLOTS)]
        out_sb = [sb(f"out_sb{i}", [L, GROUP, D]) for i in range(BUFFERS)]

        banks = [ps(f"bank{i}", [128, 512]) for i in range(4)]
        pairs = [ps(f"pair{i}", [128, 2, 512]) for i in range(2)]
        score_ps = banks[0:2]
        qkv_ps, xcT_ps = banks[2], banks[3]
        sum_ps, attnT_ps = pairs[0][:, 0, :], pairs[0][:, 1, :]
        oproj_ps, tail_ps = pairs[1][:, 0, :], pairs[1][:, 1, :]
        count_ps, held_ps = banks[2], banks[3]
        hidT_ps = banks[0:2]
        xgT_ps, down_ps = banks[2], banks[3]
        s_down_ps = banks[2:4]

        weights_in = sem("weights_in")
        expert_weights_in = sem("expert_weights_in")
        bcast_in = sem("bcast_in")
        const_made = sem("const_made")
        ident_made = sem("ident_made")
        gates_done = sem("gates_done")
        x_in = [sem(f"x_in{i}") for i in range(3)]
        c_in = sems("c_in")
        xhat_out = sems("xhat_out")
        stat_step = sem("stat_step")
        norm_step = sem("norm_step")
        xn_done = sem("xn_done")
        xcT_ready = sem("xcT_ready")
        hcT_done = sem("hcT_done")
        qkv_ready = sem("qkv_ready")
        qkv_done = sem("qkv_done")
        prod0_done = sem("prod0_done")
        prod1_done = sem("prod1_done")
        scores_ready = sem("scores_ready")
        max_done = sem("max_done")
        shifted = sem("shifted")
        exp_done = sem("exp_done")
        den_done = sem("den_done")
        rden_done = sem("rden_done")
        weighted0_done = sem("weighted0_done")
        weighted1_done = sem("weighted1_done")
        sum_ready = sem("sum_ready")
        attn_done = sem("attn_done")
        attnT_ready = sem("attnT_ready")
        attnT_done = sem("attnT_done")
        oproj_ready = sem("oproj_ready")
        x1_done = sem("x1_done")
        stat2_step = sem("stat2_step")
        norm2_step = sem("norm2_step")
        xhat_done = sem("xhat_done")
        xhatT_ready = sem("xhatT_ready")
        nT_done = sem("nT_done")
        logits_ready = sem("logits_ready")
        lg_done = sem("lg_done")

        route_step = sem("route_step")
        route_exp = sem("route_exp")
        pads_zero = sem("pads_zero")
        sums_ready = sem("sums_ready")
        counts_ready = sem("counts_ready")
        tile_expert_ready = sem("tile_expert_ready")
        onehot_step = sem("onehot_step")
        token_tile_done = sem("token_tile_done")
        column_tile_done = sem("column_tile_done")
        onehots_used = sem("onehots_used")
        held_ready = sem("held_ready")
        from_done, to_done = sem("from_done"), sem("to_done")
        gathered = sems("gathered")
        scattered = sems("scattered")
        xgT_ready = sem("xgT_ready")
        nTe_done = sem("nTe_done")
        gu_ready = sem("gu_ready")
        silu_done = sem("silu_done")
        hid_done = sem("hid_done")
        hidT_ready = sem("hidT_ready")
        hidT_done = sem("hidT_done")
        down_ready = sem("down_ready")
        y_done = sem("y_done")
        nTf_done = sem("nTf_done")
        routed_in = [sem(f"routed_in{i}") for i in range(BUFFERS)]
        s_gu_ready = sem("s_gu_ready")
        s_silu_done = sem("s_silu_done")
        s_hid_done = sem("s_hid_done")
        s_hidT_ready = sem("s_hidT_ready")
        s_hidT_done = sem("s_hidT_done")
        s_down_ready = sem("s_down_ready")
        gated_done = sem("gated_done")
        first_added = sem("first_added")
        second_added = sem("second_added")
        out_done = sem("out_done")
        out_stored = [sem(f"out_stored{i}") for i in range(BUFFERS)]

        block = ctx.enter_context(nc.Block())

        W_LOADS, EXPERT_W_LOADS = 7, 9

        class It:
            def __init__(self, i, r, total, step=SLOTS):
                self.i, self.r, self.total, self.step = i, r, total, step

            def of(self, off):
                return It(self.i, self.r + off, self.total, self.step)

            @property
            def slot(self):
                return self.r % SLOTS

            @property
            def b(self):
                return self.i * self.step + self.r

            def times(self, k, add=0):
                return self.i * (self.step * k) + (self.r * k + add)

            def round(self, k):
                return self.i * k + (self.r // self.step + 1) * k

            @property
            def inside(self):
                return not isinstance(self.i, int) or 0 <= self.b < self.total

        X_LOADS = (0, 4, 10, B)

        def batch_columns(n, width):
            return slice(n.b * width, (n.b + 1) * width) if isinstance(n.i, int) else bass.ds(n.times(width), width)

        def scores_of(s, e):
            q = qkv[s][:, 0:D].rearrange("p (l h e) -> p l h e", l=N, h=H)[:, :, :, e]
            k = qkv[s][:, D:2 * D].rearrange("p (s h e) -> p h s e", s=N, h=H)[:, :, :, e]
            return (prod[s][:, e, :].rearrange("p (l h s) -> p l h s", l=N, h=H),
                    q.unsqueeze(3).broadcast_to([L, N, H, N]), k.unsqueeze(1).broadcast_to([L, N, H, N]))

        def weighted_of(s, e):
            p = probs[s][:, :].rearrange("p (l h s) -> p s l h", l=N, h=H)
            v = qkv[s][:, 2 * D:3 * D].rearrange("p (s h e) -> p s h e", s=N, h=H)[:, :, :, e]
            return (weighted[s][:, :, :].rearrange("p s (l h e) -> p s l h e", l=N, h=H)[:, :, :, :, e],
                    p, v.unsqueeze(2).broadcast_to([L, N, N, H]))

        spare = {}

        def own_wait(eng, semaphore, value):
            if not isinstance(value, int):
                if eng.engine not in spare:
                    spare[eng.engine] = eng.alloc_register(f"spare{len(spare)}")
                eng.reg_mov(spare[eng.engine], value)
                eng.wait_ge(ident_made, 1)
                value = spare[eng.engine]
            eng.wait_ge(semaphore, value)

        def every(eng, body, begin, first, last, end, total, step=SLOTS):
            for b in range(begin, first):
                body(It(0, b, total, step))
            with eng.Fori(0, (last - first) // step) as i:
                for r in range(first, first + step):
                    body(It(i, r, total, step))
            for b in range(last, end):
                body(It(0, b, total, step))

        def every_iteration(eng, body):
            every(eng, body, -5, 7, 27, B + 3, B)

        def every_columns(eng, body):
            every(eng, body, 0, COLUMN_BUFFERS, TOP_K * B // COLUMNS, TOP_K * B // COLUMNS, TOP_K * B // COLUMNS, COLUMN_BUFFERS)

        def column_of(n, number=1, add=0):
            if isinstance(n.i, int):
                return slice(n.b + add, n.b + add + number)
            return bass.ds(n.times(1, add), number)

        T_FIRST, T_LAST = 6, TILES - 5

        def every_tile(eng, body):
            every(eng, body, -3, T_FIRST, T_LAST, TILES + 2, TILES)

        def every_batch(eng, body):
            every(eng, body, -1, BUFFERS * GROUP + 3, B - 5, B + 3, B, BUFFERS * GROUP)

        @block.sync
        def _(sp):
            def load_x(part):
                batches = slice(X_LOADS[part], X_LOADS[part + 1])
                sp.dma_start(x_all[:, :].rearrange("l (b d) -> l b d", b=B)[:, batches, :], t["x"][batches].rearrange("b l d -> l b d"))\
                    .then_inc(x_in[part], 16)

            load_x(0)
            for dst, src in ((wq, t["wq"]), (wkv, t["wkv"]), (wo, t["wo"]), (bo, t["bo"]),
                             (gamma, t["gamma"]), (beta, t["beta"]), (router, t["router"])):
                sp.dma_start(dst[:, :], src).then_inc(weights_in, 16)

            def load_expert_weights():
                for dst, src in ((ws_gu, t["ws_gu"]), (ws_dn, t["ws_dn"]), (before, t["before"]), (column_no, t["column_no"]),
                                 (token_no, t["token_no"]), (pad_id, t["pad_id"]), (iota, t["iota"].broadcast_to([L, 128]))):
                    sp.dma_start(dst[:, :], src).then_inc(expert_weights_in, 16)
                sp.dma_start(w_gu[:, :, :], t["w_gu"]).then_inc(expert_weights_in, 16)
                sp.dma_start(w_dn[:, :, :], t["w_dn"]).then_inc(expert_weights_in, 16)

            def body(it):
                if it.r == -4:
                    load_x(1)
                if it.r == -2:
                    load_x(2)
                if it.r == 1:
                    load_expert_weights()
                ld = it.of(5)
                if ld.inside:
                    if it.of(1).inside:
                        own_wait(sp, xcT_ready, it.times(1, 2))
                    sp.dma_start(cin[ld.slot][:, :], t["ctx"][ld.b]).then_inc(c_in[ld.slot], 16)
                n = it.of(-2)
                if n.inside:
                    sp.wait_ge(xhat_done, n.times(1, 1))
                    sp.dma_start(xhat_dram.rearrange("(b l) d -> b l d", l=L)[n.b], xhat[n.slot][:, :]).then_inc(xhat_out[n.slot], 16)

            every_iteration(sp, body)

            def load_routed(i, k):
                for choice in range(TOP_K):
                    sp.dma_start(yf[k][choice][:, :, :], y_of[choice, BUFFERS * i + k]).then_inc(routed_in[k], 16)

            def store(i, k):
                sp.dma_start(t["out"].rearrange("(g b) l d -> g l b d", b=GROUP)[BUFFERS * i + k], out_sb[k][:, :, :])\
                    .then_inc(out_stored[k], 16)

            y_of = y_dram[0:PAIRED, :].rearrange("(k g b l) d -> k g l b d", k=TOP_K, b=GROUP, l=L)
            for s in range(SLOTS):
                sp.wait_ge(scattered[s], 16 * ((TILES - s + SLOTS - 1) // SLOTS))
            for k in range(BUFFERS):
                load_routed(0, k)
            with sp.Fori(1, B // (BUFFERS * GROUP)) as i:
                for k in range(BUFFERS):
                    own_wait(sp, out_done, GROUP * (BUFFERS * (i - 1) + k + 1))
                    load_routed(i, k)
                    store(i - 1, k)
            for k in range(BUFFERS):
                sp.wait_ge(out_done, B - GROUP * (BUFFERS - 1 - k))
                store(B // (BUFFERS * GROUP) - 1, k)
            for k in range(BUFFERS):
                sp.wait_ge(out_stored[k], 16 * (B // (BUFFERS * GROUP)))

        @block.gpsimd
        def _(pool):
            pool.memset(ident[:, :], 0.0).then_inc(const_made, 1)
            pool.memset(minus_half[:, :], -0.5).then_inc(const_made, 1)
            pool.memset(ones[:, :], 1.0).then_inc(const_made, 1)
            pool.memset(all_ones[:, :], 1.0).then_inc(const_made, 1)
            pool.memset(zeros[:, :], 0.0).then_inc(const_made, 1)
            pool.memset(ones_bf[:, :], 1.0).then_inc(const_made, 1)
            pool.wait_ge(const_made, 6)
            pool.affine_select(out=ident[:, :], in_=ident[:, :], compare_op=ALU.not_equal, fill=1.0, base=0,
                               pattern=[[-1, 128]], channel_multiplier=1).then_inc(ident_made, 1)
            pool.dma_start(bqkv_all[:, :], t["bqkv"].broadcast_to([L, 3 * D])).then_inc(bcast_in, 16)
            for k in range(2):
                pool.dma_start(gates_in[:, k:k + 1], t["g"][:, k:k + 1].broadcast_to([L, 1])).then_inc(bcast_in, 16)

            def body(it):
                if it.inside:
                    pool.wait_ge(exp_done, it.times(1, 1))
                    pool.tensor_tensor(*weighted_of(it.slot, 1), ALU.mult).then_inc(weighted1_done, 1)
                n = it.of(2)
                if n.inside:
                    pool.wait_ge(qkv_done, n.times(1, 1))
                    pool.tensor_tensor(*scores_of(n.slot, 1), ALU.mult).then_inc(prod1_done, 1)
                n = it.of(4)
                if n.inside:
                    s = n.slot
                    own_wait(pool, stat_step, n.times(2, 2))
                    pool.tensor_scalar(vareps[s][:, :], mv[s][:, 1:2], EPS, None, ALU.add).then_inc(norm_step, 1)
                    pool.wait_ge(norm_step, n.times(3, 1))
                    pool.tensor_tensor(rstd[s][:, :], vareps[s][:, :], minus_half[:, :], ALU.pow).then_inc(norm_step, 1)
                    own_wait(pool, norm_step, n.times(3, 2))
                    pool.tensor_scalar(shift[s][:, :], mv[s][:, 0:1], rstd[s][:, 0:1], -1.0, ALU.mult, ALU.mult).then_inc(norm_step, 1)
                n = it.of(-1)
                if n.inside:
                    s = n.slot
                    own_wait(pool, stat2_step, n.times(2, 2))
                    pool.tensor_scalar(vareps2[s][:, :], mv2[s][:, 1:2], 1.0 + EPS, EPS * EPS, ALU.mult, ALU.add)\
                        .then_inc(norm2_step, 1)
                    pool.wait_ge(norm2_step, n.times(3, 1))
                    pool.tensor_tensor(rstd2[s][:, :], vareps2[s][:, :], minus_half[:, :], ALU.pow).then_inc(norm2_step, 1)
                    own_wait(pool, norm2_step, n.times(3, 2))
                    pool.tensor_scalar(shift2[s][:, :], mv2[s][:, 0:1], rstd2[s][:, 0:1], -1.0, ALU.mult, ALU.mult).then_inc(norm2_step, 1)

            every_iteration(pool, body)

            def columns(it):
                k = it.r % COLUMN_BUFFERS
                if isinstance(it.i, int):
                    which = slice(it.b * COLUMNS, (it.b + 1) * COLUMNS)
                else:
                    which = bass.ds(it.times(COLUMNS), COLUMNS)
                pool.wait_ge(onehot_step, it.times(2, 1))
                pool.tensor_tensor(column_tile[k][:, :, :], onehot_tile[k][:, :, :],
                                   column_no[:, which].unsqueeze(2).broadcast_to([L, COLUMNS, TILES]), ALU.mult).then_inc(column_tile_done, 1)

            pool.wait_ge(expert_weights_in, EXPERT_W_LOADS * 16)
            every_columns(pool, columns)

            for s in range(SLOTS):
                pool.wait_ge(xhat_out[s], 16 * (B // SLOTS))

            def tile(it):
                n = it.of(3)
                if n.inside:
                    own_wait(pool, from_done, n.times(1, 1))
                    pool.indirect_dma_start(xg[n.slot][:, :], None, xhat_dram, IndirectOffsetOnAxis(from_now[n.slot][:, :], 0))\
                        .then_inc(gathered[n.slot], 16)
                n = it.of(-2)
                if n.inside:
                    own_wait(pool, y_done, n.times(1, 1))
                    own_wait(pool, to_done, n.times(1, 1))
                    pool.indirect_dma_start(y_dram, IndirectOffsetOnAxis(to_now[n.slot][:, :], 0), y[n.slot][:, :], None)\
                        .then_inc(scattered[n.slot], 16)

            every_tile(pool, tile)

            def batch(it):
                n = it.of(-1)
                if n.inside:
                    pool.wait_ge(gated_done, n.times(1, 1))
                    if n.of(-SLOTS).inside:
                        pool.wait_ge(out_done, n.times(1, 1 - SLOTS))
                    pool.tensor_tensor(mix[n.slot][:, :], x_all[:, batch_columns(n, D)], gated[n.slot][:, :], ALU.add)\
                        .then_inc(first_added, 1)

            every_batch(pool, batch)

        @block.tensor
        def _(pe):
            pe.wait_ge(weights_in, W_LOADS * 16)
            pe.wait_ge(ident_made, 1)

            def body(it):
                n = it.of(3)
                if n.inside:
                    pe.wait_ge(c_in[n.slot], n.round(16))
                    pe.wait_ge(xn_done, n.times(1, 1))
                    if n.of(-1).inside:
                        pe.wait_ge(hcT_done, n.times(1))
                    pe.transpose(xcT_ps[:, 0:128], xn[n.slot][:, :], ident[:, :])
                    pe.transpose(xcT_ps[:, 128:256], cin[n.slot][:, :], ident[:, :]).then_inc(xcT_ready, 1)
                n = it.of(-1)
                if n.inside:
                    pe.wait_ge(attn_done, n.times(1, 1))
                    if n.of(-1).inside:
                        pe.wait_ge(attnT_done, n.times(1))
                    pe.transpose(attnT_ps[:, 0:128], attn[n.slot][:, :], ident[:, :]).then_inc(attnT_ready, 1)
                n = it.of(-1)
                if n.inside:
                    if n.of(-1).inside:
                        pe.wait_ge(x1_done, n.times(1))
                    pe.matmul(oproj_ps[:, 0:D], ones[:, :], bo[:, :], start=True, stop=False)
                    pe.wait_ge(attnT_done, n.times(1, 1))
                    pe.matmul(oproj_ps[:, 0:D], attnT[n.slot][:, :], wo[:, :], start=False, stop=True).then_inc(oproj_ready, 1)
                n = it.of(3)
                if n.inside:
                    pe.wait_ge(hcT_done, n.times(1, 1))
                    if n.of(-1).inside:
                        pe.wait_ge(qkv_done, n.times(1))
                    pe.matmul(qkv_ps[:, 0:D], hcT[n.slot][:, 0:L], wq[:, :], start=True, stop=True)
                    pe.matmul(qkv_ps[:, D:3 * D], hcT[n.slot][:, L:2 * L], wkv[:, :], start=True, stop=True).then_inc(qkv_ready, 1)
                if it.inside:
                    pe.wait_ge(weighted0_done, it.times(1, 1))
                    pe.wait_ge(weighted1_done, it.times(1, 1))
                    if it.of(-1).inside:
                        pe.wait_ge(attn_done, it.times(1))
                    for k in range(N):
                        last = pe.matmul(sum_ps[:, 0:D], ident[:, :], weighted[it.slot][:, k, :], start=(k == 0), stop=(k == N - 1))
                    last.then_inc(sum_ready, 1)
                n = it.of(-2)
                if n.inside:
                    pe.wait_ge(xhat_done, n.times(1, 1))
                    if n.of(-1).inside:
                        pe.wait_ge(lg_done, n.times(1))
                    pe.transpose(tail_ps[:, 0:128], xhat[n.slot][:, :], ident[:, :]).then_inc(xhatT_ready, 1)
                n = it.of(2)
                if n.inside:
                    pe.wait_ge(prod0_done, n.times(1, 1))
                    pe.wait_ge(prod1_done, n.times(1, 1))
                    if n.of(-2).inside:
                        pe.wait_ge(shifted, n.times(1, -1))
                    pe.matmul(score_ps[n.r % 2][:, :], ident[:, :], prod[n.slot][:, 0, :], start=True, stop=False)
                    pe.matmul(score_ps[n.r % 2][:, :], ident[:, :], prod[n.slot][:, 1, :], start=False, stop=True)\
                        .then_inc(scores_ready, 1)
                n = it.of(-2)
                if n.inside:
                    pe.wait_ge(nT_done, n.times(1, 1))
                    pe.matmul(tail_ps[:, 0:EXPERTS], nT[n.slot][:, :], router[:, :], start=True, stop=True)\
                        .then_inc(logits_ready, 1)

            every_iteration(pe, body)

            pe.wait_ge(const_made, 6)
            pe.wait_ge(expert_weights_in, EXPERT_W_LOADS * 16)
            pe.wait_ge(sums_ready, 1)
            sums = count[1][:, PAD + B - 1, :]
            pe.matmul(count_ps[:, 0:EXPERTS], before[:, :], sums, start=True, stop=True)
            pe.matmul(count_ps[:, EXPERTS:2 * EXPERTS], all_ones[:, :], sums, start=True, stop=True).then_inc(counts_ready, 1)

            pe.matmul(held_ps[:, 0:2 * TILES], ones_bf[:, :], zeros[:, :], start=True, stop=False)

            def columns(it):
                k = it.r % COLUMN_BUFFERS
                pe.wait_ge(onehot_step, it.times(2, 2))
                pe.wait_ge(token_tile_done, it.times(1, 1))
                pe.wait_ge(column_tile_done, it.times(1, 1))
                for j in range(COLUMNS):
                    pe.matmul(held_ps[:, 0:TILES], onehot_in[k][:, j, :], token_tile[k][:, j, :], start=False, stop=False)
                    last = pe.matmul(held_ps[:, TILES:2 * TILES], onehot_in[k][:, j, :], column_tile[k][:, j, :],
                                     start=False, stop=False)
                last.then_inc(onehots_used, 1)

            every_columns(pe, columns)
            pe.matmul(held_ps[:, 0:2 * TILES], ones_bf[:, :], zeros[:, :], start=False, stop=True).then_inc(held_ready, 1)

            w_gu_flat = w_gu[:, :, :].rearrange("d e f -> d (e f)")
            w_dn_flat = w_dn[:, :, :].rearrange("f c d -> f (c d)")
            front = (0, [pe.alloc_register(f"front_expert{k}") for k in range(T_FIRST)])
            looped = (T_FIRST - 3, [pe.alloc_register(f"expert{k}") for k in range(SLOTS + 3)])
            behind_loop = (T_LAST - 2, [pe.alloc_register(f"last_expert{k}") for k in range(TILES - T_LAST + 2)])

            def load_experts(held_in, n):
                pe.load(held_in[1], tile_expert[0:1, column_of(n, len(held_in[1]))])

            def expert_of(n, held_in):
                return bass.RuntimeValue.of_register_unchecked(held_in[1][n.r - held_in[0]], min_val=0, max_val=EXPERTS - 1)

            def tile(it):
                in_loop = not isinstance(it.i, int)
                experts = looped if in_loop else front if it.r < T_FIRST else behind_loop
                if it.r == -3:
                    pe.wait_ge(tile_expert_ready, 1)
                    load_experts(front, It(0, 0, TILES))
                if it.r == T_LAST:
                    load_experts(behind_loop, it.of(-2))
                n = it
                if n.inside:
                    e = expert_of(n, experts)
                    k = n.slot % 2
                    pe.wait_ge(nTe_done, n.times(1, 1))
                    if n.of(-2).inside:
                        pe.wait_ge(hid_done, n.times(1, -1))
                    pe.matmul(pairs[k][:, 0, 0:F], nTe[k][:, :], w_gu_flat[:, bass.ds(e * (2 * F), F)], start=True, stop=True)
                    pe.matmul(pairs[k][:, 1, 0:F], nTe[k][:, :], w_gu_flat[:, bass.ds(e * (2 * F) + F, F)], start=True, stop=True)\
                        .then_inc(gu_ready, 1)
                reload = it.r == T_FIRST - 1 or it.r == T_FIRST + SLOTS - 1 and in_loop
                if reload:
                    load_experts(looped, it.of(-2))
                n = it.of(1)
                if n.inside:
                    pe.wait_ge(gathered[n.slot], n.round(16))
                    if n.of(-1).inside:
                        pe.wait_ge(nTe_done, n.times(1))
                    pe.transpose(xgT_ps[:, 0:128], xg[n.slot][:, :], ident[:, :]).then_inc(xgT_ready, 1)
                n = it.of(-1)
                if n.inside:
                    k = n.slot % 2
                    pe.wait_ge(hid_done, n.times(1, 1))
                    if n.of(-2).inside:
                        pe.wait_ge(hidT_done, n.times(1, -1))
                    for c in range(FC):
                        last = pe.transpose(hidT_ps[k][:, c * 128:(c + 1) * 128], hid[k][:, c * 128:(c + 1) * 128], ident[:, :])
                    last.then_inc(hidT_ready, 1)
                n = it.of(-2)
                if n.inside:
                    e = expert_of(It(0, looped[0], TILES), looped) if reload and in_loop else expert_of(n, experts)
                    k = n.slot % 2
                    pe.wait_ge(hidT_done, n.times(1, 1))
                    if n.of(-1).inside:
                        pe.wait_ge(y_done, n.times(1))
                    for c in range(FC):
                        last = pe.matmul(down_ps[:, 0:D], hidT[k][:, c * 128:(c + 1) * 128],
                                         w_dn_flat[:, bass.ds(e * (FC * D) + c * D, D)], start=(c == 0), stop=(c == FC - 1))
                    last.then_inc(down_ready, 1)

            pe.wait_ge(from_done, 1)
            every_tile(pe, tile)

            pe.wait_ge(y_done, TILES)

            def batch(it):
                n = it
                if n.inside:
                    k = n.slot % 2
                    rows = nTf[n.slot][:, :]
                    pe.wait_ge(nTf_done, n.times(1, 1))
                    if n.of(-2).inside:
                        pe.wait_ge(s_hid_done, n.times(1, -1))
                    pe.matmul(pairs[k][:, 0, 0:FS], rows, ws_gu[:, 0:FS], start=True, stop=True)
                    pe.matmul(pairs[k][:, 1, 0:FS], rows, ws_gu[:, FS:2 * FS], start=True, stop=True)\
                        .then_inc(s_gu_ready, 1)
                n = it.of(-3)
                if n.inside:
                    k = n.slot % 2
                    pe.wait_ge(s_hidT_done, n.times(1, 1))
                    if n.of(-2).inside:
                        pe.wait_ge(out_done, n.times(1, -1))
                    pe.matmul(s_down_ps[k][:, 0:D], hidT[k][:, 0:FS], ws_dn[:, :], start=True, stop=True).then_inc(s_down_ready, 1)
                n = it.of(-1)
                if n.inside:
                    k = n.slot % 2
                    pe.wait_ge(s_hid_done, n.times(1, 1))
                    if n.of(-2).inside:
                        pe.wait_ge(s_hidT_done, n.times(1, -1))
                    pe.transpose(hidT_ps[k][:, 0:FS], hid[k][:, 0:FS], ident[:, :]).then_inc(s_hidT_ready, 1)

            every_batch(pe, batch)

        @block.scalar
        def _(act):
            def body(it):
                if it.r == 0:
                    act.wait_ge(bcast_in, 48)
                    act.activation(gates[:, :], gates_in[:, :], ACT.Tanh).then_inc(gates_done, 1)
                    act.wait_ge(weights_in, W_LOADS * 16)
                n = it.of(3)
                if n.inside:
                    s = n.slot
                    act.wait_ge(norm_step, n.times(3, 3))
                    act.activation(xn[s][:, :], x_all[:, batch_columns(n, D)], ACT.Identity, bias=shift[s][:, 0:1], scale=rstd[s][:, 0:1])\
                        .then_inc(xn_done, 1)
                n = it.of(-2)
                if n.inside:
                    s = n.slot
                    act.wait_ge(norm2_step, n.times(3, 3))
                    if n.of(-4).inside:
                        act.wait_ge(xhat_out[s], n.of(-4).round(16))
                    act.activation(xhat[s][:, :], x_all[:, batch_columns(n, D)], ACT.Identity, bias=shift2[s][:, 0:1], scale=rstd2[s][:, 0:1])\
                        .then_inc(xhat_done, 1)
                n = it.of(-1)
                if n.inside:
                    act.wait_ge(attnT_ready, n.times(1, 1))
                    act.activation(attnT[n.slot][:, :], attnT_ps[:, 0:128], ACT.Copy).then_inc(attnT_done, 1)
                n = it.of(3)
                if n.inside:
                    act.wait_ge(xcT_ready, n.times(1, 1))
                    act.activation(hcT[n.slot][:, :], xcT_ps[:, 0:256], ACT.Copy).then_inc(hcT_done, 1)
                n = it.of(-3)
                if n.inside:
                    act.wait_ge(nT_done, n.times(1, 1))
                    act.activation(nT_all[:, batch_columns(n, L)], nT[n.slot][:, :], ACT.Copy)
                n = it.of(1)
                if n.inside:
                    act.wait_ge(shifted, n.times(1, 1))
                    act.activation(probs[n.slot][:, :], probs[n.slot][:, :], ACT.Exp, scale=SM_SCALE).then_inc(exp_done, 1)
                n = it.of(-2)
                if n.inside:
                    act.wait_ge(xhatT_ready, n.times(1, 1))
                    act.activation(nT[n.slot][:, :], tail_ps[:, 0:128], ACT.Identity, bias=beta[:, 0:1], scale=gamma[:, 0:1])\
                        .then_inc(nT_done, 1)

            every_iteration(act, body)

            act.wait_ge(route_step, 2)
            act.activation(rt[1][:, :, :], rt[0][:, :, :], ACT.Exp).then_inc(route_exp, 1)
            act.wait_ge(route_step, ROUTE_GATE)
            act.activation(rs[3][:, :], rs[2][:, :], ACT.Exp).then_inc(route_exp, 1)
            act.activation(silu[0][:, 0:1], minus_half[:, :], ACT.Silu)

            def columns(it):
                k = it.r % COLUMN_BUFFERS
                act.wait_ge(onehot_step, it.times(2, 1))
                act.activation(token_tile[k][:, :, :], onehot_tile[k][:, :, :], ACT.Copy, scale=token_no[:, 0:1]).then_inc(token_tile_done, 1)

            act.wait_ge(expert_weights_in, EXPERT_W_LOADS * 16)
            every_columns(act, columns)

            def tile(it):
                n = it.of(1)
                if n.inside:
                    act.wait_ge(xgT_ready, n.times(1, 1))
                    act.activation(nTe[n.slot % 2][:, :], xgT_ps[:, 0:128], ACT.Identity, bias=beta[:, 0:1], scale=gamma[:, 0:1])\
                        .then_inc(nTe_done, 1)
                n = it
                if n.inside:
                    k = n.slot % 2
                    act.wait_ge(gu_ready, n.times(1, 1))
                    act.activation(silu[k][:, :], pairs[k][:, 0, 0:F], ACT.Silu).then_inc(silu_done, 1)
                n = it.of(-1)
                if n.inside:
                    k = n.slot % 2
                    act.wait_ge(hidT_ready, n.times(1, 1))
                    act.activation(hidT[k][:, :], hidT_ps[k][:, 0:F], ACT.Copy).then_inc(hidT_done, 1)

            every_tile(act, tile)

            def batch(it):
                n = it.of(1)
                if n.inside:
                    act.activation(nTf[n.slot][:, :], nT_all[:, batch_columns(n, L)], ACT.Copy).then_inc(nTf_done, 1)
                n = it
                if n.inside:
                    k = n.slot % 2
                    act.wait_ge(s_gu_ready, n.times(1, 1))
                    act.activation(silu[k][:, 0:FS], pairs[k][:, 0, 0:FS], ACT.Silu).then_inc(s_silu_done, 1)
                n = it.of(-1)
                if n.inside:
                    k = n.slot % 2
                    act.wait_ge(s_hidT_ready, n.times(1, 1))
                    act.activation(hidT[k][:, 0:FS], hidT_ps[k][:, 0:FS], ACT.Copy).then_inc(s_hidT_done, 1)
                n = it.of(-1)
                if n.inside:
                    group, j = n.r // GROUP % BUFFERS, n.r % GROUP
                    if j == 0:
                        act.wait_ge(routed_in[group], n.round(16 * TOP_K))
                    act.activation(gated[n.slot][:, :], yf[group][0][:, j, :], ACT.Copy, scale=pair_gate[:, column_of(n)])\
                        .then_inc(gated_done, 1)

            every_batch(act, batch)

        @block.vector
        def _(dve):
            def heads(ap):
                return ap.rearrange("p (n e) -> p n e", e=E2)

            def by_s(ap):
                return ap.rearrange("p (n s) -> p n s", s=N)

            def body(it):
                n = it.of(2)
                if n.inside:
                    if n.r == 0:
                        dve.wait_ge(bcast_in, 48)
                    dve.wait_ge(qkv_ready, n.times(1, 1))
                    dve.tensor_tensor(qkv[n.slot][:, :], qkv_ps[:, 0:3 * D], bqkv_all[:, :], ALU.add).then_inc(qkv_done, 1)
                n = it.of(-1)
                if n.inside:
                    s = n.slot
                    dve.wait_ge(sum_ready, n.times(1, 1))
                    dve.wait_ge(rden_done, n.times(1, 1))
                    dve.tensor_tensor(heads(attn[s][:, :]), heads(sum_ps[:, 0:D]), rden[s][:, :].unsqueeze(2).broadcast_to([L, NH, E2]),
                                      ALU.mult).then_inc(attn_done, 1)
                if it.inside:
                    dve.wait_ge(exp_done, it.times(1, 1))
                    dve.tensor_tensor(*weighted_of(it.slot, 0), ALU.mult).then_inc(weighted0_done, 1)
                n = it.of(2)
                if n.inside:
                    dve.wait_ge(qkv_done, n.times(1, 1))
                    dve.tensor_tensor(*scores_of(n.slot, 0), ALU.mult).then_inc(prod0_done, 1)
                n = it.of(-3)
                if n.inside:
                    logits = lg_all[:, :, :].rearrange("l b e -> l (b e)")[:, batch_columns(n, EXPERTS)]
                    dve.wait_ge(logits_ready, n.times(1, 1))
                    dve.tensor_copy(logits, tail_ps[:, 0:EXPERTS]).then_inc(lg_done, 1)
                n = it.of(4)
                if n.inside:
                    s = n.slot
                    if n.r in X_LOADS:
                        dve.wait_ge(x_in[X_LOADS.index(n.r)], 16)
                    dve.bn_stats(stats[s][:, :], x_all[:, batch_columns(n, D)]).then_inc(stat_step, 1)
                n = it.of(1)
                if n.inside:
                    s = n.slot
                    dve.wait_ge(scores_ready, n.times(1, 1))
                    dve.tensor_reduce(smax[s][:, :], by_s(score_ps[n.r % 2][:, :]), AX.X, ALU.max).then_inc(max_done, 1)
                n = it.of(4)
                if n.inside:
                    own_wait(dve, stat_step, n.times(2, 1))
                    dve.bn_aggr(mv[n.slot][:, :], stats[n.slot][:, :]).then_inc(stat_step, 1)
                n = it.of(1)
                if n.inside:
                    s = n.slot
                    dve.wait_ge(max_done, n.times(1, 1))
                    dve.tensor_tensor(by_s(probs[s][:, :]), by_s(score_ps[n.r % 2][:, :]), smax[s][:, :].unsqueeze(2).broadcast_to([L, NH, N]),
                                      ALU.subtract).then_inc(shifted, 1)
                n = it.of(-1)
                if n.inside:
                    s = n.slot
                    if n.r == 0:
                        dve.wait_ge(gates_done, 1)
                    dve.wait_ge(oproj_ready, n.times(1, 1))
                    dve.scalar_tensor_tensor(x_all[:, batch_columns(n, D)], oproj_ps[:, 0:D], gates[:, 0:1],
                                             x_all[:, batch_columns(n, D)], ALU.mult, ALU.add).then_inc(x1_done, 1)
                    own_wait(dve, x1_done, n.times(1, 1))
                    dve.bn_stats(stats2[s][:, :], x_all[:, batch_columns(n, D)]).then_inc(stat2_step, 1)
                if it.inside:
                    s = it.slot
                    dve.tensor_reduce(den[s][:, :], by_s(probs[s][:, :]), AX.X, ALU.add).then_inc(den_done, 1)
                n = it.of(-1)
                if n.inside:
                    own_wait(dve, stat2_step, n.times(2, 1))
                    dve.bn_aggr(mv2[n.slot][:, :], stats2[n.slot][:, :]).then_inc(stat2_step, 1)
                if it.inside:
                    s = it.slot
                    dve.wait_ge(den_done, it.times(1, 1))
                    dve.reciprocal(rden[s][:, :], den[s][:, :]).then_inc(rden_done, 1)

            every_iteration(dve, body)

            steps = [0]

            def step(ins):
                steps[0] += 1
                ins.then_inc(route_step, 1)
                dve.wait_ge(route_step, steps[0])

            def over_e(a):
                return a.unsqueeze(2).broadcast_to([L, B, EXPERTS])

            for e in range(EXPERTS):
                last = dve.memset(iota_e[:, e:e + 1], float(e - EXPERTS))
            for buffer in (count[0][:, 0:PAD, :], count[1][:, 0:PAD, :], tiles_of[0][:, 0:PAD_E], tiles_of[1][:, 0:PAD_E]):
                dve.memset(buffer, 0.0).then_inc(pads_zero, 1)
            dve.wait_ge(pads_zero, 4)
            by_expert = iota_e[:, :].unsqueeze(1).broadcast_to([L, B, EXPERTS])
            dve.wait_ge(lg_done, B)
            step(dve.tensor_reduce(rs[0][:, :], lg_all[:, :, :], AX.X, ALU.max))
            step(dve.tensor_tensor(rt[0][:, :, :], lg_all[:, :, :], over_e(rs[0][:, :]), ALU.subtract))
            dve.wait_ge(route_exp, 1)
            step(dve.tensor_reduce(rs[0][:, :], rt[1][:, :, :], AX.X, ALU.add))
            step(dve.reciprocal(rs[1][:, :], rs[0][:, :]))
            step(dve.tensor_tensor(rt[0][:, :, :], rt[1][:, :, :], over_e(rs[1][:, :]), ALU.mult))

            def top(p, onehot, value, scratch, index):
                step(dve.tensor_reduce(value, p, AX.X, ALU.max))
                step(dve.tensor_tensor(scratch, p, over_e(value), ALU.is_equal))
                step(dve.tensor_tensor(scratch, scratch, by_expert, ALU.mult))
                step(dve.tensor_reduce(index, scratch, AX.X, ALU.min))
                step(dve.tensor_tensor(onehot, by_expert, over_e(index), ALU.is_equal))

            top(rt[0][:, :, :], rt[2][:, :, :], rs[0][:, :], rt[1][:, :, :], rs[2][:, :])
            step(dve.scalar_tensor_tensor(rt[3][:, :, :], rt[2][:, :, :], -2.0, rt[0][:, :, :], ALU.mult, ALU.add))
            top(rt[3][:, :, :], rt[0][:, :, :], rs[1][:, :], rt[1][:, :, :], rs[2][:, :])
            step(dve.tensor_tensor(rs[2][:, :], rs[1][:, :], rs[0][:, :], ALU.subtract))
            assert steps[0] == ROUTE_GATE
            dve.wait_ge(route_exp, 2)
            step(dve.tensor_scalar(rs[0][:, :], rs[3][:, :], 1.0, None, ALU.add))
            step(dve.reciprocal(rs[1][:, :], rs[0][:, :]))
            step(dve.tensor_tensor(rs[2][:, :], rs[1][:, :], rs[3][:, :], ALU.mult))
            dve.tensor_scalar(pair_gate[:, 0:B], rs[1][:, :], gates[:, 1:2], None, ALU.mult)
            step(dve.tensor_scalar(pair_gate[:, B:2 * B], rs[2][:, :], gates[:, 1:2], None, ALU.mult))

            first, second = rt[2], rt[0]
            step(dve.tensor_tensor(count[0][:, PAD:, :], first[:, :, :], second[:, :, :], ALU.add))
            for k in range(5):
                a, b = count[k % 2], count[(k + 1) % 2]
                ins = dve.tensor_tensor(b[:, PAD:, :], a[:, PAD:, :], a[:, PAD - (1 << k):PAD + B - (1 << k), :], ALU.add)
                if k < 4:
                    step(ins)
                else:
                    ins.then_inc(sums_ready, 1)
            dve.wait_ge(sums_ready, 1)
            dve.wait_ge(counts_ready, 1)
            dve.wait_ge(expert_weights_in, EXPERT_W_LOADS * 16)
            step(dve.tensor_scalar(count_tiles[:, :], count_ps[:, EXPERTS:2 * EXPERTS], 1.0 / 128, None, ALU.mult))
            step(dve.tensor_tensor(count_over[:, :, :], count_tiles[:, :].unsqueeze(2).broadcast_to([L, EXPERTS, B]),
                                   iota[:, 0:B].unsqueeze(1).broadcast_to([L, EXPERTS, B]), ALU.is_gt))
            step(dve.tensor_reduce(tiles_of[0][:, PAD_E:], count_over[:, :, :], AX.X, ALU.add))
            for k in range(3):
                a, b = tiles_of[k % 2], tiles_of[(k + 1) % 2]
                step(dve.tensor_tensor(b[:, PAD_E:], a[:, PAD_E:], a[:, PAD_E - (1 << k):PAD_E + EXPERTS - (1 << k)], ALU.add))
            tiles_up_to = tiles_of[1]
            step(dve.scalar_tensor_tensor(first_row[:, :], tiles_up_to[:, PAD_E - 1:PAD_E + EXPERTS - 1], 128.0, count_ps[:, 0:EXPERTS],
                                          ALU.mult, ALU.add))
            step(dve.tensor_tensor(rt[1][:, :, :], count[1][:, PAD - 1:PAD + B - 1, :],
                                   first_row[:, :].unsqueeze(1).broadcast_to([L, B, EXPERTS]), ALU.add))
            for k, onehot in enumerate((first, second)):
                step(dve.tensor_tensor(rt[3][:, :, :], onehot[:, :, :], rt[1][:, :, :], ALU.mult))
                step(dve.tensor_reduce(row[:, k, :], rt[3][:, :, :], AX.X, ALU.add))
            rows = row[:, :, :].rearrange("l k b -> l (k b)")
            step(dve.tensor_scalar(row_tile[:, :], rows, 1.0 / 128, -63.5 / 128, ALU.mult, ALU.add))
            step(dve.tensor_scalar(row_in_tile[:, :], row_tile[:, :], ROUND_UP, None, ALU.add))
            step(dve.tensor_scalar(row_tile[:, :], row_in_tile[:, :], -ROUND_UP, None, ALU.add))
            step(dve.scalar_tensor_tensor(row_in_tile[:, :], row_tile[:, :], -128.0, rows, ALU.mult, ALU.add))

            def columns(it):
                k = it.r % COLUMN_BUFFERS
                if isinstance(it.i, int):
                    which = slice(it.b * COLUMNS, (it.b + 1) * COLUMNS)
                else:
                    which = bass.ds(it.times(COLUMNS), COLUMNS)

                def onehots(out, position, width):
                    shape = [L, COLUMNS, width]
                    return dve.tensor_tensor(out, position[:, which].unsqueeze(2).broadcast_to(shape),
                                             iota[:, 0:width].unsqueeze(1).broadcast_to(shape), ALU.is_equal)

                if it.of(-COLUMN_BUFFERS).inside:
                    dve.wait_ge(onehots_used, it.times(1, 1 - COLUMN_BUFFERS))
                onehots(onehot_tile[k][:, :, :], row_tile, TILES).then_inc(onehot_step, 1)
                onehots(onehot_in[k][:, :, :], row_in_tile, 128).then_inc(onehot_step, 1)

            every_columns(dve, columns)

            step(dve.tensor_tensor(behind[:, :, :], tiles_up_to[0:1, PAD_E:].unsqueeze(1).broadcast_to([1, TILES, EXPERTS]),
                                   iota[0:1, 0:TILES].unsqueeze(2).broadcast_to([1, TILES, EXPERTS]), ALU.is_le))
            step(dve.tensor_reduce(tile_expert_f[:, :], behind[:, :, :], AX.X, ALU.add))
            step(dve.tensor_scalar(tile_expert_f[:, :], tile_expert_f[:, :], EXPERTS - 1.0, None, ALU.min))
            dve.tensor_copy(tile_expert[:, :], tile_expert_f[:, :]).then_inc(tile_expert_ready, 1)
            dve.wait_ge(held_ready, 1)
            pair, second_off, pad_to, src, dst = (h[:, :] for h in held)
            step(dve.tensor_scalar(src, held_ps[:, 0:TILES], -1.0, None, ALU.add))
            step(dve.scalar_tensor_tensor(pair, held_ps[:, TILES:2 * TILES], 128.0, src, ALU.mult, ALU.add))
            step(dve.tensor_scalar(second_off, pair, float(TOKENS), -float(TOKENS), ALU.is_ge, ALU.mult))
            step(dve.tensor_tensor(src, pair, second_off, ALU.add))
            step(dve.tensor_scalar(src, src, 0.0, TOKENS - 1.0, ALU.max, ALU.min))
            step(dve.tensor_copy(from_row[:, :], src))

            def output_rows():
                step(dve.scalar_tensor_tensor(pad_to, pair, 0.0, pad_id[:, :], ALU.is_lt, ALU.mult))
                step(dve.tensor_tensor(dst, pair, pad_to, ALU.add))
                step(dve.tensor_scalar(dst, dst, 0.0, Y_ROWS - 1.0, ALU.max, ALU.min))
                step(dve.tensor_copy(to_row[:, :], dst))

            def tile(it):
                if it.r == 0 and isinstance(it.i, int):
                    output_rows()
                n = it.of(3)
                if n.inside:
                    dve.tensor_copy(from_now[n.slot][:, :], from_row[:, column_of(n)]).then_inc(from_done, 1)
                n = it.of(-2)
                if n.inside:
                    s = n.slot
                    if n.of(-4).inside:
                        dve.wait_ge(scattered[s], n.of(-4).round(16))
                    dve.tensor_copy(to_now[s][:, :], to_row[:, column_of(n)]).then_inc(to_done, 1)
                    dve.wait_ge(down_ready, n.times(1, 1))
                    dve.tensor_copy(y[s][:, :], down_ps[:, 0:D]).then_inc(y_done, 1)
                n = it
                if n.inside:
                    k = n.slot % 2
                    dve.wait_ge(silu_done, n.times(1, 1))
                    dve.tensor_tensor(hid[k][:, :], pairs[k][:, 1, 0:F], silu[k][:, :], ALU.mult).then_inc(hid_done, 1)

            every_tile(dve, tile)

            def batch(it):
                n = it
                if n.inside:
                    k = n.slot % 2
                    dve.wait_ge(s_silu_done, n.times(1, 1))
                    dve.tensor_tensor(hid[k][:, 0:FS], pairs[k][:, 1, 0:FS], silu[k][:, 0:FS], ALU.mult).then_inc(s_hid_done, 1)
                n = it.of(-3)
                if n.inside:
                    group, j = n.r // GROUP % BUFFERS, n.r % GROUP
                    dve.wait_ge(s_down_ready, n.times(1, 1))
                    dve.wait_ge(second_added, n.times(1, 1))
                    if j == 0 and n.of(-BUFFERS * GROUP).inside:
                        dve.wait_ge(out_stored[group], n.of(-BUFFERS * GROUP).round(16))
                    dve.scalar_tensor_tensor(out_sb[group][:, j, :], s_down_ps[n.slot % 2][:, 0:D], gates[:, 1:2],
                                             mix[n.slot][:, :], ALU.mult, ALU.add).then_inc(out_done, 1)
                n = it.of(-2)
                if n.inside:
                    group, j = n.r // GROUP % BUFFERS, n.r % GROUP
                    if j == 0:
                        dve.wait_ge(routed_in[group], n.round(16 * TOP_K))
                    dve.wait_ge(first_added, n.times(1, 1))
                    dve.scalar_tensor_tensor(mix[n.slot][:, :], yf[group][1][:, j, :], pair_gate[:, column_of(n, add=B)],
                                             mix[n.slot][:, :], ALU.mult, ALU.add).then_inc(second_added, 1)

            every_batch(dve, batch)


ROUTE_GATE = 17


def kernel(**inputs):
    import concourse.bacc as bacc
    from concourse.bass_utils import run_bass_kernel_spmd

    a = {k: np.asarray(v) for k, v in inputs.items()}
    gu = a["L0_ffn_gate_up_w"]
    arrays = {
        "x": a["x"], "ctx": a["ctx_1024"],
        "g": np.concatenate([a["g_xattn"], a["g_ffn"]]).reshape(1, 2),
        "wq": a["L0_xattn_Wq"].T, "wkv": np.concatenate([a["L0_xattn_Wk"], a["L0_xattn_Wv"]]).T,
        "bqkv": np.concatenate([a["L0_xattn_bq"], a["L0_xattn_bk"], a["L0_xattn_bv"]]).reshape(1, 3 * D),
        "wo": a["L0_xattn_Wo"].T, "bo": a["L0_xattn_bo"].reshape(1, D),
        "gamma": a["L0_ffn_ln_gamma"].reshape(D, 1), "beta": a["L0_ffn_ln_beta"].reshape(D, 1),
        "router": a["L0_ffn_router_w"].T,
        "w_gu": gu.transpose(2, 0, 1),
        "w_dn": a["L0_ffn_down_w"].transpose(0, 2, 1).reshape(EXPERTS, FC, 128, D).transpose(2, 0, 1, 3).reshape(128, EXPERTS * FC, D),
        "before": np.triu(np.ones((128, 128), np.float32), 1), "iota": np.arange(128, dtype=np.float32).reshape(1, 128),
        "column_no": np.tile(np.arange(TOP_K * B, dtype=np.float32), (L, 1)),
        "token_no": (np.arange(L) + 1).astype(np.float32).reshape(L, 1),
        "pad_id": (PAIRED + np.arange(TILES)[None, :] * 128 + np.arange(128)[:, None] + 1).astype(np.float32),
        "ws_gu": a["L0_ffn_shared_gate_up_w"].T, "ws_dn": a["L0_ffn_shared_down_w"].T,
    }
    nc = bacc.Bacc("TRN2", target_bir_lowering=False, num_devices=1)
    fed, t = {}, {}
    for name, v in arrays.items():
        v = np.ascontiguousarray(v)
        fed[f"in_{name}"] = v
        t[name] = nc.dram_tensor(f"in_{name}", v.shape, mybir.dt.from_np(v.dtype), kind="ExternalInput").ap()
    t["out"] = nc.dram_tensor("out", [B, L, D], FP32, kind="ExternalOutput").ap()
    attention_then_moe(nc, t)
    r = run_bass_kernel_spmd(nc, [fed], core_ids=[0])
    return r.results[0]["out"]
```
